# Optimizing a Trainium2 kernel written in Bass

```python
import numpy as np
import jax
import jax.numpy as jnp

def _softmax(x, axis=-1):
    return jax.nn.softmax(x, axis=axis)

def _gelu(x):
    return jax.nn.gelu(x, approximate=True)

def _silu(x):
    return jax.nn.silu(x)

def _sigmoid(x):
    return jax.nn.sigmoid(x)

def _layernorm(x, axis=-1, eps=1e-05):
    m = jnp.mean(x, axis=axis, keepdims=True)
    v = jnp.var(x, axis=axis, keepdims=True)
    return (x - m) / jnp.sqrt(v + eps)

def _scatter_add(tgt, idx, src, axis=0):
    return tgt.at[idx].add(src)

def _segment_sum(src, seg, n):
    return jax.ops.segment_sum(src, seg, n)
kernel_name = 'mk_adaln_d1_jaxref_r4_a71008'

def setup_inputs(seed: int=0):
    np.random.seed(seed)
    _w = jnp.asarray

    def _L0_attn_setup():
        import jax, jax.numpy as jnp
        import numpy as np
        B, T, D, H = (4, 512, 256, 16)
        HD = D // H
        EPS = 1e-06

        def _phi(x):
            return jax.nn.elu(x) + 1.0

        def _linear_attn(x, Wq, bq, Wk, bk, Wv, bv, Wo, bo):
            b, t, d = x.shape

            def proj(W, bias):
                y = x @ W.T + bias
                return y.reshape(b, t, H, HD).transpose(0, 2, 1, 3)
            qp = _phi(proj(Wq, bq))
            kp = _phi(proj(Wk, bk))
            v = proj(Wv, bv)
            q_tm = qp.transpose(2, 0, 1, 3)
            k_tm = kp.transpose(2, 0, 1, 3)
            v_tm = v.transpose(2, 0, 1, 3)
            kv0 = jnp.zeros((b, H, HD, HD), dtype=x.dtype)
            ks0 = jnp.zeros((b, H, HD), dtype=x.dtype)

            def step(carry, inp):
                kv, ksum = carry
                kt, vt, qt = inp
                kv = kv + jnp.einsum('bhd,bhe->bhde', kt, vt)
                ksum = ksum + kt
                num = jnp.einsum('bhd,bhde->bhe', qt, kv)
                den = jnp.einsum('bhd,bhd->bh', qt, ksum)[..., None] + EPS
                return ((kv, ksum), num / den)
            _, out_tm = jax.lax.scan(step, (kv0, ks0), (k_tm, v_tm, q_tm))
            out = out_tm.transpose(1, 0, 2, 3).reshape(b, t, d)
            return out @ Wo.T + bo
        key = jax.random.key(seed)
        ks = jax.random.split(key, 9)
        s = 1.0 / np.sqrt(D)
        return {'x': jax.random.normal(ks[0], (B, T, D), dtype=jnp.float32), 'Wq': jax.random.normal(ks[1], (D, D), dtype=jnp.float32) * s, 'bq': jnp.zeros((D,), dtype=jnp.float32), 'Wk': jax.random.normal(ks[2], (D, D), dtype=jnp.float32) * s, 'bk': jnp.zeros((D,), dtype=jnp.float32), 'Wv': jax.random.normal(ks[3], (D, D), dtype=jnp.float32) * s, 'bv': jnp.zeros((D,), dtype=jnp.float32), 'Wo': jax.random.normal(ks[4], (D, D), dtype=jnp.float32) * s, 'bo': jnp.zeros((D,), dtype=jnp.float32)}
    _L0_attn_in = _L0_attn_setup()

    def _L0_ffn_setup():
        import jax, jax.numpy as jnp
        import numpy as np
        DIM = 256
        DEPTH = 2
        HEADS = 8
        DIM_HEAD = 64
        WINDOW = 128
        INNER = HEADS * DIM_HEAD
        HID = int(DIM * 4 * 2 / 3)
        B, N = (2, 2048)
        QK_SCALE = 8.0

        def shift_token(t):
            t1, t2 = jnp.split(t, 2, axis=-1)
            t2 = jnp.pad(t2, ((0, 0), (1, 0), (0, 0)))[:, :-1]
            return jnp.concatenate([t1, t2], axis=-1)

        def l2norm(t):
            return t / jnp.clip(jnp.linalg.norm(t, axis=-1, keepdims=True), 1e-12)

        def rotate_half(x):
            x1, x2 = jnp.split(x, 2, axis=-1)
            return jnp.concatenate([-x2, x1], axis=-1)

        def rotary_xpos(q, k):
            n = q.shape[-2]
            half_idx = jnp.arange(0, DIM_HEAD, 2, dtype=jnp.float32)
            inv_freq = 1.0 / 10000.0 ** (half_idx / DIM_HEAD)
            t = jnp.arange(n, dtype=jnp.float32)
            freqs = t[:, None] * inv_freq[None, :]
            freqs = jnp.concatenate([freqs, freqs], axis=-1)
            base = (half_idx + 0.4 * DIM_HEAD) / (1.4 * DIM_HEAD)
            power = (t - n // 2) / float(WINDOW // 2)
            scale = base[None, :] ** power[:, None]
            scale = jnp.concatenate([scale, scale], axis=-1)
            cos, sin = (jnp.cos(freqs), jnp.sin(freqs))
            q = q * cos * scale + rotate_half(q) * sin * scale
            k = k * cos / scale + rotate_half(k) * sin / scale
            return (q, k)

        def local_attention(q, k, v):
            b, h, n, d = q.shape
            w = n // WINDOW
            bq = q.reshape(b, h, w, WINDOW, d) * QK_SCALE
            bk = k.reshape(b, h, w, WINDOW, d)
            bv = v.reshape(b, h, w, WINDOW, d)

            def look_around(t):
                p = jnp.pad(t, ((0, 0), (0, 0), (1, 0), (0, 0), (0, 0)))
                return jnp.concatenate([p[:, :, :w], p[:, :, 1:]], axis=3)
            bk, bv = (look_around(bk), look_around(bv))
            bt = jnp.arange(n).reshape(w, WINDOW)
            btp = jnp.pad(bt, ((1, 0), (0, 0)), constant_values=-1)
            btk = jnp.concatenate([btp[:w], btp[1:]], axis=1)
            sim = jnp.einsum('bhwid,bhwjd->bhwij', bq, bk)
            i = bt[:, :, None]
            j = btk[:, None, :]
            mask = (i < j) | (i > j + WINDOW) | (j == -1)
            sim = jnp.where(mask, -jnp.finfo(sim.dtype).max, sim)
            attn = jax.nn.softmax(sim, axis=-1)
            out = jnp.einsum('bhwij,bhwjd->bhwid', attn, bv)
            return out.reshape(b, h, n, d)

        def _layer(x, wqkv, qs, ksc, wo, lg, lb, w1, b1, w2, b2):
            b, n, _ = x.shape
            h = shift_token(x)
            qkv = h @ wqkv
            q, k, v = jnp.split(qkv, 3, axis=-1)
            to_heads = lambda t: t.reshape(b, n, HEADS, DIM_HEAD).transpose(0, 2, 1, 3)
            q, k, v = (to_heads(q), to_heads(k), to_heads(v))
            q = l2norm(q) * qs
            k = l2norm(k) * ksc
            q, k = rotary_xpos(q, k)
            o = local_attention(q, k, v)
            o = o.transpose(0, 2, 1, 3).reshape(b, n, INNER)
            x = x + o @ wo
            h = shift_token(x)
            mu = h.mean(-1, keepdims=True)
            var = h.var(-1, keepdims=True)
            h = (h - mu) / jnp.sqrt(var + 1e-05) * lg + lb
            h = h @ w1 + b1
            a, g = jnp.split(h, 2, axis=-1)
            h = a * jax.nn.gelu(g, approximate=False)
            x = x + h @ w2 + b2
            return x
        key = jax.random.key(seed)
        ks = jax.random.split(key, 6)
        return {'x': jax.random.normal(ks[0], (B, N, DIM), jnp.float32), 'wqkv': jax.random.normal(ks[1], (DEPTH, DIM, 3 * INNER), jnp.float32) * 0.02, 'q_scale': jnp.ones((DEPTH, DIM_HEAD), jnp.float32), 'k_scale': jnp.ones((DEPTH, DIM_HEAD), jnp.float32), 'wo': jax.random.normal(ks[2], (DEPTH, INNER, DIM), jnp.float32) * 0.02, 'ln_g': jnp.ones((DEPTH, DIM), jnp.float32), 'ln_b': jnp.zeros((DEPTH, DIM), jnp.float32), 'w1': jax.random.normal(ks[3], (DEPTH, DIM, 2 * HID), jnp.float32) * 0.02, 'b1': jnp.zeros((DEPTH, 2 * HID), jnp.float32), 'w2': jax.random.normal(ks[4], (DEPTH, HID, DIM), jnp.float32) * 0.02, 'b2': jnp.zeros((DEPTH, DIM), jnp.float32)}
    _L0_ffn_in = _L0_ffn_setup()
    _L0_c = _w((lambda *s: np.random.randn(*s).astype(np.float32) * 0.05)(8, 256))
    _L0_wmod = _w((lambda *s: np.random.randn(*s).astype(np.float32) * 0.05)(256, 6 * 256) * 256 ** (-0.5))
    _d = {'L0_attn_x': _L0_attn_in['x'], 'L0_attn_Wq': _L0_attn_in['Wq'], 'L0_attn_bq': _L0_attn_in['bq'], 'L0_attn_Wk': _L0_attn_in['Wk'], 'L0_attn_bk': _L0_attn_in['bk'], 'L0_attn_Wv': _L0_attn_in['Wv'], 'L0_attn_bv': _L0_attn_in['bv'], 'L0_attn_Wo': _L0_attn_in['Wo'], 'L0_attn_bo': _L0_attn_in['bo'], 'L0_ffn_wqkv': _L0_ffn_in['wqkv'], 'L0_ffn_q_scale': _L0_ffn_in['q_scale'], 'L0_ffn_k_scale': _L0_ffn_in['k_scale'], 'L0_ffn_wo': _L0_ffn_in['wo'], 'L0_ffn_ln_g': _L0_ffn_in['ln_g'], 'L0_ffn_ln_b': _L0_ffn_in['ln_b'], 'L0_ffn_w1': _L0_ffn_in['w1'], 'L0_ffn_b1': _L0_ffn_in['b1'], 'L0_ffn_w2': _L0_ffn_in['w2'], 'L0_ffn_b2': _L0_ffn_in['b2'], 'L0_c': _L0_c, 'L0_wmod': _L0_wmod}
    _x0 = _d['L0_attn_x']
    _d['L0_attn_x'] = jax.random.normal(jax.random.fold_in(jax.random.key(seed), 1), (8, 1024, 256), dtype=_x0.dtype)
    del _x0
    return _d

def reference(L0_attn_x, L0_attn_Wq, L0_attn_bq, L0_attn_Wk, L0_attn_bk, L0_attn_Wv, L0_attn_bv, L0_attn_Wo, L0_attn_bo, L0_ffn_wqkv, L0_ffn_q_scale, L0_ffn_k_scale, L0_ffn_wo, L0_ffn_ln_g, L0_ffn_ln_b, L0_ffn_w1, L0_ffn_b1, L0_ffn_w2, L0_ffn_b2, L0_c, L0_wmod):

    def _L0_attn_ref(x, Wq, bq, Wk, bk, Wv, bv, Wo, bo):
        import jax, jax.numpy as jnp
        import numpy as np
        B, T, D, H = (4, 512, 256, 16)
        HD = D // H
        EPS = 1e-06

        def _phi(x):
            return jax.nn.elu(x) + 1.0

        def _linear_attn(x, Wq, bq, Wk, bk, Wv, bv, Wo, bo):
            b, t, d = x.shape

            def proj(W, bias):
                y = x @ W.T + bias
                return y.reshape(b, t, H, HD).transpose(0, 2, 1, 3)
            qp = _phi(proj(Wq, bq))
            kp = _phi(proj(Wk, bk))
            v = proj(Wv, bv)
            q_tm = qp.transpose(2, 0, 1, 3)
            k_tm = kp.transpose(2, 0, 1, 3)
            v_tm = v.transpose(2, 0, 1, 3)
            kv0 = jnp.zeros((b, H, HD, HD), dtype=x.dtype)
            ks0 = jnp.zeros((b, H, HD), dtype=x.dtype)

            def step(carry, inp):
                kv, ksum = carry
                kt, vt, qt = inp
                kv = kv + jnp.einsum('bhd,bhe->bhde', kt, vt)
                ksum = ksum + kt
                num = jnp.einsum('bhd,bhde->bhe', qt, kv)
                den = jnp.einsum('bhd,bhd->bh', qt, ksum)[..., None] + EPS
                return ((kv, ksum), num / den)
            _, out_tm = jax.lax.scan(step, (kv0, ks0), (k_tm, v_tm, q_tm))
            out = out_tm.transpose(1, 0, 2, 3).reshape(b, t, d)
            return out @ Wo.T + bo
        return _linear_attn(x, Wq, bq, Wk, bk, Wv, bv, Wo, bo)

    def _L0_ffn_ref(x, wqkv, q_scale, k_scale, wo, ln_g, ln_b, w1, b1, w2, b2):
        import jax, jax.numpy as jnp
        import numpy as np
        DIM = 256
        DEPTH = 2
        HEADS = 8
        DIM_HEAD = 64
        WINDOW = 128
        INNER = HEADS * DIM_HEAD
        HID = int(DIM * 4 * 2 / 3)
        B, N = (2, 2048)
        QK_SCALE = 8.0

        def shift_token(t):
            t1, t2 = jnp.split(t, 2, axis=-1)
            t2 = jnp.pad(t2, ((0, 0), (1, 0), (0, 0)))[:, :-1]
            return jnp.concatenate([t1, t2], axis=-1)

        def l2norm(t):
            return t / jnp.clip(jnp.linalg.norm(t, axis=-1, keepdims=True), 1e-12)

        def rotate_half(x):
            x1, x2 = jnp.split(x, 2, axis=-1)
            return jnp.concatenate([-x2, x1], axis=-1)

        def rotary_xpos(q, k):
            n = q.shape[-2]
            half_idx = jnp.arange(0, DIM_HEAD, 2, dtype=jnp.float32)
            inv_freq = 1.0 / 10000.0 ** (half_idx / DIM_HEAD)
            t = jnp.arange(n, dtype=jnp.float32)
            freqs = t[:, None] * inv_freq[None, :]
            freqs = jnp.concatenate([freqs, freqs], axis=-1)
            base = (half_idx + 0.4 * DIM_HEAD) / (1.4 * DIM_HEAD)
            power = (t - n // 2) / float(WINDOW // 2)
            scale = base[None, :] ** power[:, None]
            scale = jnp.concatenate([scale, scale], axis=-1)
            cos, sin = (jnp.cos(freqs), jnp.sin(freqs))
            q = q * cos * scale + rotate_half(q) * sin * scale
            k = k * cos / scale + rotate_half(k) * sin / scale
            return (q, k)

        def local_attention(q, k, v):
            b, h, n, d = q.shape
            w = n // WINDOW
            bq = q.reshape(b, h, w, WINDOW, d) * QK_SCALE
            bk = k.reshape(b, h, w, WINDOW, d)
            bv = v.reshape(b, h, w, WINDOW, d)

            def look_around(t):
                p = jnp.pad(t, ((0, 0), (0, 0), (1, 0), (0, 0), (0, 0)))
                return jnp.concatenate([p[:, :, :w], p[:, :, 1:]], axis=3)
            bk, bv = (look_around(bk), look_around(bv))
            bt = jnp.arange(n).reshape(w, WINDOW)
            btp = jnp.pad(bt, ((1, 0), (0, 0)), constant_values=-1)
            btk = jnp.concatenate([btp[:w], btp[1:]], axis=1)
            sim = jnp.einsum('bhwid,bhwjd->bhwij', bq, bk)
            i = bt[:, :, None]
            j = btk[:, None, :]
            mask = (i < j) | (i > j + WINDOW) | (j == -1)
            sim = jnp.where(mask, -jnp.finfo(sim.dtype).max, sim)
            attn = jax.nn.softmax(sim, axis=-1)
            out = jnp.einsum('bhwij,bhwjd->bhwid', attn, bv)
            return out.reshape(b, h, n, d)

        def _layer(x, wqkv, qs, ksc, wo, lg, lb, w1, b1, w2, b2):
            b, n, _ = x.shape
            h = shift_token(x)
            qkv = h @ wqkv
            q, k, v = jnp.split(qkv, 3, axis=-1)
            to_heads = lambda t: t.reshape(b, n, HEADS, DIM_HEAD).transpose(0, 2, 1, 3)
            q, k, v = (to_heads(q), to_heads(k), to_heads(v))
            q = l2norm(q) * qs
            k = l2norm(k) * ksc
            q, k = rotary_xpos(q, k)
            o = local_attention(q, k, v)
            o = o.transpose(0, 2, 1, 3).reshape(b, n, INNER)
            x = x + o @ wo
            h = shift_token(x)
            mu = h.mean(-1, keepdims=True)
            var = h.var(-1, keepdims=True)
            h = (h - mu) / jnp.sqrt(var + 1e-05) * lg + lb
            h = h @ w1 + b1
            a, g = jnp.split(h, 2, axis=-1)
            h = a * jax.nn.gelu(g, approximate=False)
            x = x + h @ w2 + b2
            return x
        for l in range(DEPTH):
            x = _layer(x, wqkv[l], q_scale[l], k_scale[l], wo[l], ln_g[l], ln_b[l], w1[l], b1[l], w2[l], b2[l])
        return x
    x = L0_attn_x
    mod = (_silu(L0_c) @ L0_wmod).reshape(L0_c.shape[0], 6, 1, -1)
    sa, ca, ga, sb, cb, gb = (mod[:, 0], mod[:, 1], mod[:, 2], mod[:, 3], mod[:, 4], mod[:, 5])
    ga = (2 * (ga >= 0) - 1) * jnp.maximum(jnp.abs(ga), 0.25)
    gb = (2 * (gb >= 0) - 1) * jnp.maximum(jnp.abs(gb), 0.25)
    h = _layernorm(x, axis=-1) * (1 + ca) + sa
    x = x + ga * _L0_attn_ref(h, L0_attn_Wq, L0_attn_bq, L0_attn_Wk, L0_attn_bk, L0_attn_Wv, L0_attn_bv, L0_attn_Wo, L0_attn_bo)
    h = _layernorm(x, axis=-1) * (1 + cb) + sb
    x = x + gb * _L0_ffn_ref(h, L0_ffn_wqkv, L0_ffn_q_scale, L0_ffn_k_scale, L0_ffn_wo, L0_ffn_ln_g, L0_ffn_ln_b, L0_ffn_w1, L0_ffn_b1, L0_ffn_w2, L0_ffn_b2)
    return x

_drawn_inputs = setup_inputs


def setup_inputs(seed=0):
    import zlib

    import numpy as np

    out = dict(_drawn_inputs(seed))
    spreads = {'L0_attn_bq': (0.0, 2.0),
     'L0_attn_bk': (0.0, 2.0),
     'L0_attn_bv': (0.0, 0.33),
     'L0_attn_bo': (0.0, 0.33),
     'L0_ffn_q_scale': (1.0, 0.6),
     'L0_ffn_k_scale': (1.0, 0.6),
     'L0_ffn_ln_g': (1.0, 0.6),
     'L0_ffn_ln_b': (0.0, 0.8),
     'L0_ffn_b1': (0.0, 0.8),
     'L0_ffn_b2': (0.0, 0.518)}
    factors = {'L0_attn_Wq': 8.0,
     'L0_attn_Wk': 8.0,
     'L0_ffn_wqkv': 6.759,
     'L0_ffn_wo': 6.626,
     'L0_ffn_w1': 4.771,
     'L0_ffn_w2': 4.751}
    for name, (base, spread) in spreads.items():
        noise = np.random.default_rng([zlib.crc32(name.encode()), seed]).standard_normal(out[name].shape)
        drawn = base * np.exp(spread * noise) if base else spread * noise
        out[name] = jnp.asarray(drawn.astype(out[name].dtype))
    for name, factor in factors.items():
        out[name] = (out[name] * factor).astype(out[name].dtype)
    return out
```

```python
from contextlib import ExitStack

import numpy as np

import concourse.bass as bass
from concourse import mybir

F32 = mybir.dt.float32
BF16 = mybir.dt.bfloat16
I32 = mybir.dt.int32
ALU = mybir.AluOpType
ACT = mybir.ActivationFunctionType
AX = mybir.AxisListType

P = 128
D = 256
KC = D // P
STREAMS = 2
AH, AD, PAD = 16, 16, 32
AC = AH * PAD // P
AG = P // PAD
AV = AD + 1
DEPTH, LH, LD = 2, 8, 64
INNER = LH * LD
PAIRS = LH // 2
LV = LD + 1
HID = 682
HC = -(-HID // P)
LAST = HID - (HC - 1) * P
WINDOW = 128
MASKED = -1e30
EPS_LN, EPS_DEN = 1e-5, 1e-6
MAGIC = float(0x5F3759DF)

FILLS_A = [("z", 0), ("qk", 1), ("v", 2), ("qT", 3), ("kT", 0),
           ("score0", 1), ("score1", 2), ("score2", 3), ("score3", 1), ("num", 0), ("kv", 2),
           ("o", 3), ("wo", 0)]
FILLS_L = [("x", 1), ("q", 2), ("k", 3), ("v", 0), ("qT", 1), ("kT", 0),
           ("sim0", 1), ("sim1", 2), ("p0", 0), ("sim2", 1), ("p1", 0), ("sim3", 2), ("p2", 0), ("o0", 3),
           ("p3", 0), ("o1", 3), ("o", 0), ("wo", 1), ("z", 2), ("ag0", 3), ("ag1", 0), ("ag2", 1), ("w2", 2)]


def bank_turns():
    turn, count = {}, [0] * 4
    for key, bank in [(("A", k), b) for k, b in FILLS_A] + [((l, k), b) for l in range(DEPTH) for k, b in FILLS_L]:
        turn[key] = (bank, count[bank])
        count[bank] += 1
    return turn, count


TURN, FILLS = bank_turns()
CHAIN = 100


def adaln_block(nc, x, waT, woaT, ba, bo, wqkv, qs, ks, wo, ln_g, ln_b, w1, b1, w2, b2, cT, wmod,
                rotary, ident, causal, blockdiag, window, out):
    B = cT.shape[1]
    STREAM_TILES = out.shape[1]
    ROUNDS = B // STREAMS
    TILES = STREAM_TILES // ROUNDS

    mod_dram = nc.dram_tensor("mod_rows", (B, 6 * D), F32, kind="Internal").ap()

    with ExitStack() as ctx:
        def sb(name, shape, dt=F32):
            return ctx.enter_context(nc.sbuf_tensor(name, shape, dt))

        def sem(name):
            return ctx.enter_context(nc.semaphore(name))

        def each(make, name, *a):
            return [make(f"{name}_{s}", *a) for s in range(STREAMS)]

        WA = sb("WA", [P, KC, 3 * D])
        WOA = sb("WOA", [P, KC, D])
        WQKV = sb("WQKV", [P, DEPTH, KC, 3 * INNER])
        WO = sb("WO", [P, DEPTH, INNER // P, D])
        W1 = sb("W1", [P, DEPTH, KC, 2 * HID])
        W2 = sb("W2", [P, DEPTH, HC, D])
        BA = sb("BA", [P, 3 * D])
        BO = sb("BO", [P, D])
        B2 = sb("B2", [P, DEPTH * D])
        B1 = sb("B1", [P, DEPTH * 2 * HC])
        LN = sb("LN", [P, 2 * DEPTH * KC])
        ROT = sb("ROT", [P, DEPTH, TILES, 2, 2, LD])
        IDENT = sb("IDENT", [P, P])
        IDENTB = sb("IDENTB", [P, P], BF16)
        CAUSAL = sb("CAUSAL", [P, P])
        ZERO = sb("ZERO", [P, 1])
        BLOCKDIAG = sb("BLOCKDIAG", [P, AC * AG * AV])
        WINDOWB = sb("WINDOWB", [P, 2, 2 * 2 * WINDOW], BF16)

        xin = each(sb, "xin", [P, D])
        x1 = each(sb, "x1", [P, D])
        xl = each(sb, "xl", [P, D])
        mod = each(sb, "mod", [P, 4 * D])
        modT = each(sb, "modT", [P, 2 * KC])
        state = each(sb, "state", [P, AC * AG * AV])
        tailcol = each(sb, "tailcol", [P, DEPTH])
        tailrow = each(sb, "tailrow", [1, DEPTH, P])
        kprev = each(sb, "kprev", [P, DEPTH, PAIRS, P])
        vprev = each(sb, "vprev", [P, DEPTH, LH, LV])
        st = each(sb, "st", [P, 2, 6])
        mv = each(sb, "mv", [P, 2])
        rs = each(sb, "rs", [P, 4, 2 * LH])
        z = each(sb, "z", [P, D])
        zT = each(sb, "zT", [P, KC, P + 1])
        v1 = each(sb, "v1", [P, AH, AV])
        vw = each(sb, "vw", [P, LH, LV])
        mx = each(sb, "mx", [P, 2, LH])
        rd = each(sb, "rd", [P, 2, AH])
        xs2 = each(sb, "xs2", [P, P])
        spare = each(sb, "spare", [P, 1])
        y = each(sb, "y", [P, D])

        SCRATCH = 6400
        scratch = each(sb, "scratch", [P, SCRATCH])

        def carve(at, *shape):
            n = int(np.prod(shape))
            assert at + n <= SCRATCH
            names = " ".join("abcd"[:len(shape)])
            sizes = dict(zip("bcd", shape[1:]))
            return [t[:, at:at + n].rearrange(f"p ({names}) -> p {names}", **sizes) for t in scratch]

        qkb = carve(0, 2 * AH, AD)
        ex = carve(512, 2 * AH, AD)
        below = carve(1024, 2 * AH, AD)
        oa = carve(0, AH, AD)
        oaT = carve(256, KC, P)
        t0 = carve(512, AC * AG * AV)
        phi = carve(1536, 2, AC, AG, PAD)
        phiT = carve(2560, 2, AC, P)
        sm = carve(3584, AG, AC, P)
        sq = carve(0, 2, LH, LD)
        rot1 = carve(1024, 2, LH, LD)
        rot2 = carve(2048, 2, LH, LD)
        qk = carve(3072, 2, PAIRS, P)
        qT = carve(4096, PAIRS, P)
        kT = carve(4608, PAIRS, P)
        pr = carve(0, 2, 4, WINDOW)
        pT = carve(1024, 2, 4, P)
        on = carve(2048, INNER // P, P)
        oT = carve(2560, INNER // P, P)
        gl = carve(0, HC, P)
        hid = carve(768, HC, P)
        xb = carve(1536, D)

        bank = [[ctx.enter_context(nc.psum_tensor(f"bank_{s}_{b}", [P, 512], F32)) for b in range(4)]
                for s in range(STREAMS)]

        filled = [[sem(f"filled_{s}_{b}") for b in range(4)] for s in range(STREAMS)]
        drained = [[sem(f"drained_{s}_{b}") for b in range(4)] for s in range(STREAMS)]
        modulation_loaded, weights_loaded, rotary_loaded = sem("modulation_loaded"), sem("weights_loaded"), sem("rotary_loaded")
        silu_ready, gate_step, modrow_full, modrow_ready, mod_stored = (
            sem("silu_ready"), sem("gate_step"), sem("modrow_full"), sem("modrow_ready"), sem("mod_stored"))
        consts_ready, factors_ready = sem("consts_ready"), sem("factors_ready")
        xin_loaded, mod_loaded, tails_zeroed, state_zeroed = (
            each(sem, "xin_loaded"), each(sem, "mod_loaded"), each(sem, "tails_zeroed"), each(sem, "state_zeroed"))
        chain = each(sem, "vector_chain")
        z_ready = each(sem, "z_ready")
        exp_ready, below_ready, phi_ready, state_ready, x1_ready, xl_ready, y_ready, y_stored = (
            each(sem, "exp_ready"), each(sem, "below_ready"), each(sem, "phi_ready"), each(sem, "state_ready"),
            each(sem, "x1_ready"), each(sem, "xl_ready"), each(sem, "y_ready"), each(sem, "y_stored"))
        squares_ready = each(sem, "squares_ready")
        q_ready, ksum_ready, knorm_ready, k_ready = (
            each(sem, "q_ready"), each(sem, "ksum_ready"), each(sem, "knorm_ready"), each(sem, "k_ready"))
        negmax_ready = each(sem, "negmax_ready")
        kv_moved = each(sem, "kv_moved")
        tail_read, tail_saved, shifted = each(sem, "tail_read"), each(sem, "tail_saved"), each(sem, "shifted")
        tail_used = each(sem, "tail_used")
        gelu_ready = each(sem, "gelu_ready")
        xb_ready = each(sem, "xb_ready")

        def heads_of(m):
            return [4 * (m // 2) + m % 2 + 2 * k for k in range(2)]

        def held(s, key):
            return bank[s][TURN[key][0]]

        def wait_free(eng, s, n, key):
            b, turn = TURN[key]
            eng.wait_ge(drained[s][b], n * FILLS[b] + turn)

        def wait_filled(eng, s, n, key):
            b, turn = TURN[key]
            eng.wait_ge(filled[s][b], n * FILLS[b] + (turn + 1))

        def wait_drained(eng, s, n, key):
            b, turn = TURN[key]
            eng.wait_ge(drained[s][b], n * FILLS[b] + (turn + 1))

        def fill(s, key):
            return filled[s][TURN[key][0]]

        def drain(s, key):
            return drained[s][TURN[key][0]]

        WEIGHT_LOADS = 8 + 5 * DEPTH + 5
        NCONST = 12

        WM = [ROT[:, l].rearrange("p t q f d -> p (t q f d)")[:, 0:6 * D] for l in range(DEPTH)]
        crow = z[0][:, 0:KC * B]
        srow = z[1][:, 0:KC * B]
        modrow = scratch[0][0:B, 0:6 * D]
        modtmp = scratch[0][0:B, 6 * D:8 * D]
        scales = y[0][:, 0:DEPTH * 2 * LD].rearrange("p (l q d) -> p l q d", l=DEPTH, q=2)
        windowf = scratch[1][:, 0:2 * 4 * WINDOW]

        block = ctx.enter_context(nc.Block())

        @block.sync
        def _(sp):
            count = [0]

            def load(dst, src):
                sp.dma_start(dst, src).then_inc(weights_loaded, 16)
                count[0] += 1

            sp.dma_start(crow.rearrange("p (c b) -> p c b", c=KC), cT.rearrange("(c p) b -> p c b", p=P)).then_inc(modulation_loaded, 16)
            for c in range(KC):
                sp.dma_start(WM[c], wmod[c * P:(c + 1) * P]).then_inc(modulation_loaded, 16)
            for s in range(STREAMS):
                sp.dma_start(xin[s][:], x[s, 0]).then_inc(xin_loaded[s], 16)
            load(IDENT[:], ident)
            load(WA[:], waT.rearrange("(c p) n -> p c n", p=P))
            load(BA[:], ba.partition_broadcast(P).rearrange("p o n -> p (o n)"))
            load(CAUSAL[:], causal)
            load(BLOCKDIAG[:], blockdiag)
            load(WOA[:], woaT.rearrange("(c p) n -> p c n", p=P))
            load(BO[:], bo.partition_broadcast(P).rearrange("p o n -> p (o n)"))
            load(windowf, window)
            for l in range(DEPTH):
                load(WQKV[:, l], wqkv[l].rearrange("(c p) n -> p c n", p=P))
                load(WO[:, l], wo[l].rearrange("(c p) n -> p c n", p=P))
                load(W1[:, l], w1[l].rearrange("(c p) n -> p c n", p=P))
                load(W2[:, l, 0:HC - 1], w2[l, 0:(HC - 1) * P].rearrange("(c p) n -> p c n", p=P))
                load(W2[0:LAST, l, HC - 1], w2[l, (HC - 1) * P:HID])
            load(B2[:], b2.partition_broadcast(P).rearrange("p o n -> p (o n)"))
            load(B1[:], b1)
            load(LN[:], ln_g)
            load(scales[:, :, 0], qs.partition_broadcast(P))
            load(scales[:, :, 1], ks.partition_broadcast(P))
            assert count[0] == WEIGHT_LOADS
            sp.wait_ge(modrow_full, 3)
            for l in range(DEPTH):
                sp.dma_start(ROT[:, l].rearrange("p t q f d -> p (t q f d)"), rotary).then_inc(rotary_loaded, 16)
            sp.wait_ge(modrow_ready, 6)
            sp.dma_start(mod_dram, modrow).then_inc(mod_stored, 16)

            with sp.Fori(0, ROUNDS) as j:
                with sp.Fori(0, TILES) as i:
                    n = j * TILES + i
                    for s in range(STREAMS):
                        sp.wait_ge(x1_ready[s], n + 1)
                        sp.dma_start(xin[s][:], x[s, bass.ds(n + 1, 1)].rearrange("o p d -> (o p) d")).then_inc(xin_loaded[s], 16)
                    for l in range(DEPTH):
                        for s in range(STREAMS):
                            if l == 0:
                                sp.wait_ge(tails_zeroed[s], j + 1)
                                sp.wait_ge(tail_saved[s], j * (TILES * 16 * DEPTH) + i * (16 * DEPTH))
                                sp.wait_ge(z_ready[s], n * 3 + 1)
                            else:
                                sp.wait_ge(z_ready[s], n * 3 + (1 + l))
                                sp.wait_ge(tail_saved[s], n * (16 * DEPTH) + 16 * l)
                            sp.dma_start(xs2[s][0:1, :], tailrow[s][:, l]).then_inc(tail_read[s], 16)
                        for s in range(STREAMS):
                            wait_drained(sp, s, n, (l, "wo"))
                            sp.dma_start(xs2[s][1:P, :], xl[s][0:P - 1, P:D]).then_inc(shifted[s], 16)
                            sp.wait_ge(tail_read[s], n * (16 * DEPTH) + 16 * (l + 1))
                            sp.dma_start(tailrow[s][:, l], xl[s][P - 1:P, P:D]).then_inc(tail_saved[s], 16)
                    for s in range(STREAMS):
                        sp.wait_ge(y_ready[s], n + 1)
                        sp.dma_start(out[s, bass.ds(n, 1)].rearrange("o p d -> (o p) d"), y[s][:]).then_inc(y_stored[s], 16)
            for s in range(STREAMS):
                sp.wait_ge(y_stored[s], 16 * STREAM_TILES)
                sp.wait_ge(xin_loaded[s], 16 * (STREAM_TILES + 1))
                sp.wait_ge(tail_saved[s], 16 * DEPTH * STREAM_TILES)

        @block.tensor
        def _(pe):
            def project(s, n, key, lhsT, rhs, cols, rows=P):
                wait_free(pe, s, n, key)
                for c in range(len(lhsT)):
                    mm = nc.tensor.matmul(held(s, key)[0:rows, 0:cols], lhsT[c], rhs[c],
                                          start=(c == 0), stop=(c == len(lhsT) - 1))
                mm.then_inc(fill(s, key), 1)

            def turn(s, n, key, blocks):
                wait_free(pe, s, n, key)
                for k, b in enumerate(blocks):
                    mm = nc.tensor.transpose(held(s, key)[:, k * P:(k + 1) * P], b, IDENT[:])
                mm.then_inc(fill(s, key), 1)

            def halves(t):
                return [t[:, c * P:(c + 1) * P] for c in range(KC)]

            pe.wait_ge(modulation_loaded, 48)
            pe.wait_ge(silu_ready, 1)
            for k in range(3):
                for c in range(KC):
                    mm = nc.tensor.matmul(bank[0][k][0:B, :], srow[:, c * B:(c + 1) * B], WM[c][:, k * 512:(k + 1) * 512],
                                          start=(c == 0), stop=(c == KC - 1))
                mm.then_inc(modrow_full, 1)
            pe.wait_ge(weights_loaded, 16 * WEIGHT_LOADS)
            pe.wait_ge(consts_ready, NCONST)
            pe.wait_ge(modrow_ready, 6)

            with pe.Fori(0, ROUNDS) as j:
                with pe.Fori(0, TILES) as i:
                    n = j * TILES + i

                    def a_turn_z(s):
                        pe.wait_ge(z_ready[s], n * 3 + 1)
                        turn(s, n, ("A", "z"), halves(z[s]))

                    def a_project(s):
                        wait_drained(pe, s, n, ("A", "z"))
                        h = [zT[s][:, c, 0:P] for c in range(KC)]
                        project(s, n, ("A", "qk"), h, [WA[:, c, 0:2 * D] for c in range(KC)], 2 * D)
                        project(s, n, ("A", "v"), h, [WA[:, c, 2 * D:] for c in range(KC)], D)

                    def a_turn_phi(s):
                        pe.wait_ge(phi_ready[s], n + 1)
                        for q, key in enumerate(("qT", "kT")):
                            turn(s, n, ("A", key), [phi[s][:, q, c].rearrange("p g d -> p (g d)") for c in range(AC)])

                    def a_scores(s):
                        wait_drained(pe, s, n, ("A", "qT"))
                        wait_drained(pe, s, n, ("A", "kT"))
                        for g in range(AG):
                            key = ("A", f"score{g}")
                            wait_free(pe, s, n, key)
                            rows = slice(g * PAD, g * PAD + AD)
                            for c in range(AC):
                                mm = nc.tensor.matmul(held(s, key)[:, c * P:(c + 1) * P], phiT[s][rows, 1, c], phiT[s][rows, 0, c],
                                                      start=True, stop=True)
                            mm.then_inc(fill(s, key), 1)

                    def a_numerators(s):
                        key = ("A", "num")
                        wait_free(pe, s, n, key)
                        pe.wait_ge(state_ready[s], n)
                        pe.wait_ge(state_zeroed[s], j + 1)
                        acc = held(s, key)
                        for c in range(AC):
                            w = AG * AV
                            nc.tensor.matmul(acc[:, c * w:(c + 1) * w], phiT[s][:, 0, c], state[s][:, c * w:(c + 1) * w],
                                             start=(c == 0), stop=False, skip_group_check=True)
                        wait_drained(pe, s, n, ("A", "v"))
                        for g in range(AG):
                            wait_drained(pe, s, n, ("A", f"score{g}"))
                            for c in range(AC):
                                h = c * AG + g
                                mm = nc.tensor.matmul(acc[:, h * AV:(h + 1) * AV], sm[s][:, g, c], v1[s][:, h],
                                                      start=False, stop=(h == AH - 1), skip_group_check=True)
                        mm.then_inc(fill(s, key), 1)
                        key = ("A", "kv")
                        wait_free(pe, s, n, key)
                        for c in range(AC):
                            w = AG * AV
                            mm = nc.tensor.matmul(held(s, key)[:, c * w:(c + 1) * w],
                                                  phi[s][:, 1, c].rearrange("p g d -> p (g d)"),
                                                  v1[s][:, c * AG:(c + 1) * AG].rearrange("p h d -> p (h d)"), start=True, stop=True)
                        mm.then_inc(fill(s, key), 1)

                    def a_turn_o(s):
                        wait_drained(pe, s, n, ("A", "num"))
                        flat = oa[s].rearrange("p h d -> p (h d)")
                        turn(s, n, ("A", "o"), halves(flat))

                    def a_out(s):
                        wait_drained(pe, s, n, ("A", "o"))
                        project(s, n, ("A", "wo"), [oaT[s][:, c] for c in range(KC)], [WOA[:, c] for c in range(KC)], D)

                    def turn_x(s, l):
                        if l == 0:
                            pe.wait_ge(xl_ready[s], n + 1)
                        else:
                            wait_drained(pe, s, n, (l - 1, "w2"))
                        turn(s, n, (l, "x"), halves(xl[s]))

                    def project_qkv(s, l):
                        wait_drained(pe, s, n, (l, "x"))
                        xs = [zT[s][:, c, 0:P] for c in range(KC)]
                        for k, key in enumerate("qkv"):
                            project(s, n, (l, key), xs, [WQKV[:, l, c, k * INNER:(k + 1) * INNER] for c in range(KC)], INNER)

                    def turn_qk(s, l):
                        pe.wait_ge(q_ready[s], n * DEPTH + (l + 1))
                        turn(s, n, (l, "qT"), [qk[s][:, 0, p] for p in range(PAIRS)])
                        pe.wait_ge(k_ready[s], n * DEPTH + (l + 1))
                        turn(s, n, (l, "kT"), [qk[s][:, 1, p] for p in range(PAIRS)])

                    def sim(s, l, p):
                        if p == 0:
                            wait_drained(pe, s, n, (l, "kT"))
                            pe.wait_ge(kv_moved[s], n * (2 * DEPTH) + 2 * l)
                        key = (l, f"sim{p}")
                        wait_free(pe, s, n, key)
                        first = (i + (TILES - 1)) // TILES
                        nc.tensor.matmul(held(s, key)[:], IDENTB[:], WINDOWB[:, bass.ds(first, 1)].rearrange("p o n -> p (o n)"),
                                         start=True, stop=False, skip_group_check=True)
                        rows = slice(p % 2 * LD, (p % 2 + 1) * LD)
                        for e, h in enumerate(heads_of(p)):
                            for kb, keys in enumerate((kprev[s][rows, l, h // 2], kT[s][rows, h // 2])):
                                col = (2 * e + kb) * WINDOW
                                mm = nc.tensor.matmul(held(s, key)[:, col:col + WINDOW], qT[s][rows, h // 2], keys,
                                                      start=False, stop=(e == 1 and kb == 1), skip_group_check=True)
                        mm.then_inc(fill(s, key), 1)

                    def turn_p(s, l, p):
                        wait_drained(pe, s, n, (l, f"sim{p}"))
                        turn(s, n, (l, f"p{p}"), [pr[s][:, p % 2, k] for k in range(4)])

                    def weigh_v(s, l, p):
                        key = (l, f"o{p // 2}")
                        if p % 2 == 0:
                            wait_free(pe, s, n, key)
                        wait_drained(pe, s, n, (l, f"p{p}"))
                        for e, h in enumerate(heads_of(p)):
                            col = (h % 4) * LV
                            for kb, values in enumerate((vprev[s][:, l, h], vw[s][:, h])):
                                mm = nc.tensor.matmul(held(s, key)[:, col:col + LV], pT[s][:, p % 2, 2 * e + kb], values,
                                                      start=(p % 2 == 0 and e == 0 and kb == 0),
                                                      stop=(p % 2 == 1 and e == 1 and kb == 1), skip_group_check=True)
                        if p % 2 == 1:
                            mm.then_inc(fill(s, key), 1)

                    def turn_o(s, l):
                        wait_drained(pe, s, n, (l, "o1"))
                        turn(s, n, (l, "o"), [on[s][:, c] for c in range(INNER // P)])

                    def project_o(s, l):
                        wait_drained(pe, s, n, (l, "o"))
                        project(s, n, (l, "wo"), [oT[s][:, c] for c in range(INNER // P)], [WO[:, l, c] for c in range(INNER // P)], D)

                    def turn_z(s, l):
                        pe.wait_ge(z_ready[s], n * 3 + (2 + l))
                        turn(s, n, (l, "z"), halves(z[s]))

                    def widen(s, l):
                        wait_drained(pe, s, n, (l, "z"))
                        for m in range(HC // 2):
                            key = (l, f"ag{m}")
                            wait_free(pe, s, n, key)
                            for k in range(2):
                                rows = LAST if 2 * m + k == HC - 1 else P
                                for g in range(2):
                                    at = g * HID + (2 * m + k) * P
                                    for c in range(KC):
                                        mm = nc.tensor.matmul(held(s, key)[0:rows, (2 * k + g) * P:(2 * k + g + 1) * P],
                                                              W1[:, l, c, at:at + rows], zT[s][:, c, 0:P],
                                                              start=(c == 0), stop=(c == KC - 1))
                            mm.then_inc(fill(s, key), 1)

                    def narrow(s, l):
                        key = (l, "w2")
                        wait_free(pe, s, n, key)
                        for m in range(HC):
                            if m % 2 == 0:
                                wait_drained(pe, s, n, (l, f"ag{m // 2}"))
                            rows = LAST if m == HC - 1 else P
                            mm = nc.tensor.matmul(held(s, key)[:, 0:D], hid[s][0:rows, m], W2[0:rows, l, m],
                                                  start=(m == 0), stop=(m == HC - 1))
                        mm.then_inc(fill(s, key), 1)

                    for step in (a_turn_z, a_project, a_turn_phi, a_scores, a_numerators, a_turn_o, a_out):
                        for s in range(STREAMS):
                            step(s)
                    for l in range(DEPTH):
                        for step in (turn_x, project_qkv, turn_qk):
                            for s in range(STREAMS):
                                step(s, l)
                        for s in range(STREAMS):
                            sim(s, l, 0)
                            sim(s, l, 1)
                        for p in range(PAIRS):
                            for s in range(STREAMS):
                                turn_p(s, l, p)
                                if p + 2 < PAIRS:
                                    sim(s, l, p + 2)
                                if p >= 1:
                                    weigh_v(s, l, p - 1)
                        for s in range(STREAMS):
                            weigh_v(s, l, PAIRS - 1)
                        for step in (turn_o, project_o, turn_z, widen, narrow):
                            for s in range(STREAMS):
                                step(s, l)

        @block.scalar
        def _(act):
            act.wait_ge(modulation_loaded, 48)
            nc.scalar.activation(srow, crow, ACT.Silu).then_inc(silu_ready, 1)
            act.wait_ge(weights_loaded, 16 * WEIGHT_LOADS)
            act.wait_ge(consts_ready, NCONST)
            act.wait_ge(mod_stored, 16)

            def copy(dst, src):
                return nc.scalar.activation(dst, src, ACT.Copy)

            with act.Fori(0, ROUNDS) as j:
                for s in range(STREAMS):
                    act.wait_ge(y_ready[s], j * TILES)
                    row = mod_dram[bass.ds(j * STREAMS + s, 1)]
                    act.dma_start(mod[s][:], row[:, 2 * D:].partition_broadcast(P).rearrange("p o d -> p (o d)")).then_inc(mod_loaded[s], 16)
                    with nc.allow_non_contiguous_dma(reason="two rows of 256 for each batch element, one to a partition"):
                        act.dma_start(modT[s][:], row[:, 0:2 * D].rearrange("o (r p) -> p (o r)", p=P)).then_inc(mod_loaded[s], 16)
                for s in range(STREAMS):
                    act.wait_ge(mod_loaded[s], j * 32 + 32)
                    act.wait_ge(tails_zeroed[s], j + 1)
                with act.Fori(0, TILES) as i:
                    n = j * TILES + i

                    def affine_z(s, key, scale, bias):
                        wait_filled(act, s, n, key)
                        for c in range(KC):
                            ins = nc.scalar.activation(zT[s][:, c, 0:P], held(s, key)[:, c * P:(c + 1) * P], ACT.Identity,
                                                       scale=scale[c], bias=bias[c])
                        ins.then_inc(drain(s, key), 1)

                    def a_h(s):
                        affine_z(s, ("A", "z"), [modT[s][:, KC + c:KC + c + 1] for c in range(KC)],
                                 [modT[s][:, c:c + 1] for c in range(KC)])

                    def a_exp(s):
                        act.wait_ge(below_ready[s], n + 1)
                        nc.scalar.activation(ex[s][:], below[s][:], ACT.Exp).then_inc(exp_ready[s], 1)

                    def a_phiT(s):
                        for q, key in enumerate(("qT", "kT")):
                            wait_filled(act, s, n, ("A", key))
                            copy(phiT[s][:, q].rearrange("p c t -> p (c t)"), held(s, ("A", key))[:]).then_inc(drain(s, ("A", key)), 1)

                    def a_oT(s):
                        wait_filled(act, s, n, ("A", "o"))
                        copy(oaT[s].rearrange("p c t -> p (c t)"), held(s, ("A", "o"))[:, 0:D]).then_inc(drain(s, ("A", "o")), 1)

                    def shift_x(s, l):
                        key = (l, "x")
                        wait_filled(act, s, n, key)
                        copy(zT[s][:, 1, 0:1], tailcol[s][:, l:l + 1]).then_inc(tail_used[s], 1)
                        copy(zT[s][:, 0, 0:P], held(s, key)[:, 0:P])
                        copy(zT[s][:, 1, 1:P + 1], held(s, key)[:, P:2 * P])
                        act.wait_ge(tail_used[s], n * DEPTH + (l + 1))
                        copy(tailcol[s][:, l:l + 1], held(s, key)[:, 2 * P - 1:2 * P]).then_inc(drain(s, key), 1)

                    def squares(s, l):
                        for q, key in enumerate("qk"):
                            wait_filled(act, s, n, (l, key))
                            nc.scalar.activation(sq[s][:, q].rearrange("p h d -> p (h d)"), held(s, (l, key))[:],
                                                 ACT.Square).then_inc(squares_ready[s], 1)
                        wait_filled(act, s, n, (l, "v"))
                        act.wait_ge(kv_moved[s], n * (2 * DEPTH) + 2 * l)
                        copy(vw[s][:, :, 0:LD], held(s, (l, "v"))[:].rearrange("p (h d) -> p h d", h=LH)).then_inc(drain(s, (l, "v")), 1)

                    def qkT(s, l):
                        for key, dst in (("qT", qT), ("kT", kT)):
                            wait_filled(act, s, n, (l, key))
                            copy(dst[s].rearrange("p a t -> p (a t)"), held(s, (l, key))[:]).then_inc(drain(s, (l, key)), 1)

                    def probs(s, l, p):
                        key = (l, f"sim{p}")
                        act.wait_ge(negmax_ready[s], n * (PAIRS * DEPTH) + (PAIRS * l + p + 1))
                        for e, h in enumerate(heads_of(p)):
                            ins = nc.scalar.activation(pr[s][:, p % 2, 2 * e:2 * e + 2].rearrange("p a t -> p (a t)"),
                                                       held(s, key)[:, e * 2 * WINDOW:(e + 1) * 2 * WINDOW], ACT.Exp,
                                                       scale=rs[s][:, 3, h:h + 1], bias=mx[s][:, 1, h:h + 1])
                        ins.then_inc(drain(s, key), 1)

                    def turned_p(s, l, p):
                        key = (l, f"p{p}")
                        wait_filled(act, s, n, key)
                        copy(pT[s][:, p % 2].rearrange("p a t -> p (a t)"), held(s, key)[:]).then_inc(drain(s, key), 1)

                    def turned_o(s, l):
                        wait_filled(act, s, n, (l, "o"))
                        copy(oT[s].rearrange("p c t -> p (c t)"), held(s, (l, "o"))[:]).then_inc(drain(s, (l, "o")), 1)

                    def affine(s, l):
                        g = (l * 2) * KC
                        affine_z(s, (l, "z"), [LN[:, g + c:g + c + 1] for c in range(KC)],
                                 [LN[:, g + KC + c:g + KC + c + 1] for c in range(KC)])

                    def gelus(s, l):
                        for m in range(HC):
                            key = (l, f"ag{m // 2}")
                            if m % 2 == 0:
                                wait_filled(act, s, n, key)
                            rows = LAST if m == HC - 1 else P
                            b = (l * 2 + 1) * HC + m
                            at = (2 * (m % 2) + 1) * P
                            nc.scalar.activation(gl[s][0:rows, m], held(s, key)[0:rows, at:at + P], ACT.Gelu,
                                                 bias=B1[0:rows, b:b + 1]).then_inc(gelu_ready[s], 1)

                    for step in (a_h, a_exp, a_phiT, a_oT):
                        for s in range(STREAMS):
                            step(s)
                    for l in range(DEPTH):
                        for step in (shift_x, squares, qkT):
                            for s in range(STREAMS):
                                step(s, l)
                        for s in range(STREAMS):
                            probs(s, l, 0)
                            probs(s, l, 1)
                        for p in range(PAIRS):
                            for s in range(STREAMS):
                                if p % 2 == 1:
                                    turned_p(s, l, p)
                                if p + 2 < PAIRS:
                                    probs(s, l, p + 2)
                        for step in (turned_o, affine, gelus):
                            for s in range(STREAMS):
                                step(s, l)

        @block.vector
        def _(dve):
            V = nc.vector

            V.memset(ZERO[:], 0.0).then_inc(consts_ready, 1)
            for s in range(STREAMS):
                V.memset(kprev[s][:], 0.0).then_inc(consts_ready, 1)
                V.memset(vprev[s][:], 0.0).then_inc(consts_ready, 1)
                V.memset(v1[s][:], 1.0).then_inc(consts_ready, 1)
                V.memset(vw[s][:], 1.0).then_inc(consts_ready, 1)
            dve.wait_ge(modrow_full, 3)
            for k in range(6):
                src = bank[0][k // 2][0:B, (k % 2) * D:(k % 2 + 1) * D]
                dst = modrow[:, k * D:(k + 1) * D]
                if k in (0, 3):
                    V.tensor_copy(dst, src).then_inc(modrow_ready, 1)
                elif k in (1, 4):
                    V.tensor_scalar(dst, src, 1.0, None, ALU.add).then_inc(modrow_ready, 1)
                else:
                    before = 3 * (k // 3)
                    if k == 5:
                        dve.wait_ge(modrow_ready, 5)
                    V.tensor_scalar(modtmp[:, 0:D], src, 0.0, 2.0, ALU.is_ge, ALU.mult).then_inc(gate_step, 1)
                    V.tensor_scalar(modtmp[:, D:2 * D], src, -1.0, 0.25, ALU.mult, ALU.max).then_inc(gate_step, 1)
                    dve.wait_ge(gate_step, before + 2)
                    V.tensor_tensor(modtmp[:, D:2 * D], src, modtmp[:, D:2 * D], ALU.max).then_inc(gate_step, 1)
                    dve.wait_ge(gate_step, before + 3)
                    V.scalar_tensor_tensor(out=dst, in0=modtmp[:, 0:D], scalar=-1.0, in1=modtmp[:, D:2 * D],
                                           op0=ALU.add, op1=ALU.mult).then_inc(modrow_ready, 1)
            dve.wait_ge(weights_loaded, 16 * WEIGHT_LOADS)
            V.tensor_copy(IDENTB[:], IDENT[:]).then_inc(consts_ready, 1)
            V.tensor_copy(WINDOWB[:].rearrange("p f n -> p (f n)"), windowf).then_inc(consts_ready, 1)
            dve.wait_ge(consts_ready, 11)
            dve.wait_ge(mod_stored, 16)
            for s in range(STREAMS):
                ins = V.memset(scratch[s][:], 0.0)
            ins.then_inc(consts_ready, 1)
            dve.wait_ge(factors_ready, 4 * DEPTH)
            dve.wait_ge(consts_ready, NCONST)

            with dve.Fori(0, ROUNDS) as j:
                for s in range(STREAMS):
                    V.memset(state[s][:], 0.0).then_inc(state_zeroed[s], 1)
                    dve.wait_ge(tail_saved[s], j * (16 * DEPTH * TILES))
                    V.memset(tailcol[s][:], 0.0)
                    V.memset(tailrow[s][:], 0.0).then_inc(tails_zeroed[s], 1)
                with dve.Fori(0, TILES) as i:
                    n = j * TILES + i
                    links = [0] * STREAMS

                    def link(s, ins):
                        links[s] += 1
                        ins.then_inc(chain[s], 1)
                        dve.wait_ge(chain[s], n * CHAIN + links[s])

                    def rsqrt(s, k, floor=None, eps=None):
                        v, r, t = (rs[s][:, a, 0:k] for a in range(3))
                        link(s, V.tensor_scalar(t.bitcast(I32), v.bitcast(I32), 1, None, ALU.logical_shift_right))
                        link(s, V.tensor_scalar(r.bitcast(I32), t.bitcast(I32), -1.0, MAGIC, ALU.mult, ALU.add))
                        for _ in range(3):
                            link(s, V.tensor_tensor(t, r, r, ALU.mult))
                            link(s, V.scalar_tensor_tensor(out=t, in0=t, scalar=-0.5, in1=v, op0=ALU.mult, op1=ALU.mult))
                            link(s, V.scalar_tensor_tensor(out=r, in0=t, scalar=1.5, in1=r, op0=ALU.add, op1=ALU.mult))

                    def normalise(s, parts):
                        for k, part in enumerate(parts):
                            ins = V.bn_stats(st[s][:, k], part)
                        link(s, ins)
                        V.memset(spare[s][:], 0.0)
                        link(s, V.bn_aggr(mv[s][:], st[s][:, 0:len(parts)].rearrange("p a b -> p (a b)")))
                        link(s, V.tensor_scalar(rs[s][:, 0, 0:1], mv[s][:, 1:2], EPS_LN, None, ALU.add))
                        rsqrt(s, 1)
                        at = 0
                        for part in parts:
                            w = part.shape[1]
                            ins = V.tensor_scalar(z[s][:, at:at + w], part, mv[s][:, 0:1], rs[s][:, 1, 0:1],
                                                  ALU.subtract, ALU.mult)
                            at += w
                        return ins

                    def a_norm(s):
                        dve.wait_ge(xin_loaded[s], n * 16 + 16)
                        normalise(s, [xin[s][:]]).then_inc(z_ready[s], 1)

                    def a_bias(s):
                        wait_filled(dve, s, n, ("A", "qk"))
                        V.tensor_tensor(qkb[s].rearrange("p h d -> p (h d)"), held(s, ("A", "qk"))[:], BA[:, 0:2 * D],
                                        ALU.add).then_inc(drain(s, ("A", "qk")), 1)
                        wait_drained(dve, s, n, ("A", "qk"))
                        V.tensor_scalar(below[s][:], qkb[s][:], 0.0, None, ALU.min).then_inc(below_ready[s], 1)
                        wait_filled(dve, s, n, ("A", "v"))
                        V.tensor_tensor(v1[s][:, :, 0:AD], held(s, ("A", "v"))[:, 0:D].rearrange("p (h d) -> p h d", h=AH),
                                        BA[:, 2 * D:].rearrange("p (h d) -> p h d", h=AH), ALU.add).then_inc(drain(s, ("A", "v")), 1)

                    def a_phi(s):
                        dve.wait_ge(exp_ready[s], n + 1)
                        V.scalar_tensor_tensor(out=phi[s].rearrange("p q c g d -> p (q c g) d")[:, :, 0:AD], in0=qkb[s][:], scalar=0.0,
                                               in1=ex[s][:], op0=ALU.max, op1=ALU.add).then_inc(phi_ready[s], 1)

                    def a_mask(s):
                        for g in range(AG):
                            key = ("A", f"score{g}")
                            wait_filled(dve, s, n, key)
                            V.tensor_tensor(sm[s][:, g], held(s, key)[:].rearrange("p (c t) -> p c t", c=AC),
                                            CAUSAL[:].unsqueeze(1).to_broadcast((P, AC, P)), ALU.mult).then_inc(drain(s, key), 1)

                    def a_divide(s):
                        key = ("A", "num")
                        wait_filled(dve, s, n, key)
                        num = held(s, key)[:, 0:AH * AV].rearrange("p (h d) -> p h d", h=AH)
                        link(s, V.tensor_scalar(rd[s][:, 0].unsqueeze(2), num[:, :, AD:AV], EPS_DEN, None, ALU.add))
                        link(s, V.reciprocal(rd[s][:, 1], rd[s][:, 0]))
                        V.tensor_tensor(oa[s][:], num[:, :, 0:AD], rd[s][:, 1].unsqueeze(2).to_broadcast((P, AH, AD)),
                                        ALU.mult).then_inc(drain(s, key), 1)
                        key = ("A", "kv")
                        wait_filled(dve, s, n, key)
                        V.tensor_tensor(t0[s][:], held(s, key)[:, 0:AH * AV], BLOCKDIAG[:], ALU.mult).then_inc(drain(s, key), 1)
                        wait_drained(dve, s, n, key)
                        V.tensor_tensor(state[s][:], state[s][:], t0[s][:], ALU.add).then_inc(state_ready[s], 1)

                    def a_add(s):
                        key = ("A", "wo")
                        wait_filled(dve, s, n, key)
                        dve.wait_ge(mod_loaded[s], j * 32 + 32)
                        V.tensor_tensor(t0[s][:, 0:D], held(s, key)[:, 0:D], BO[:], ALU.add).then_inc(drain(s, key), 1)
                        wait_drained(dve, s, n, key)
                        link(s, V.tensor_tensor(t0[s][:, 0:D], t0[s][:, 0:D], mod[s][:, 0:D], ALU.mult))
                        V.tensor_tensor(x1[s][:], t0[s][:, 0:D], xin[s][:], ALU.add).then_inc(x1_ready[s], 1)

                    def modulate(s):
                        dve.wait_ge(x1_ready[s], n + 1)
                        link(s, normalise(s, [x1[s][:]]))
                        link(s, V.tensor_tensor(z[s][:], z[s][:], mod[s][:, 2 * D:3 * D], ALU.mult))
                        V.tensor_tensor(xl[s][:], z[s][:], mod[s][:, D:2 * D], ALU.add).then_inc(xl_ready[s], 1)

                    def rotate(s, l):
                        for q, key in enumerate("qk"):
                            got = held(s, (l, key))[:]
                            factor = [ROT[:, l, bass.ds(i, 1), q, f] for f in range(2)]
                            dve.wait_ge(squares_ready[s], n * (2 * DEPTH) + (2 * l + q + 1))
                            V.tensor_tensor(rot1[s][:, q], got.rearrange("p (h d) -> p h d", h=LH),
                                            factor[0].to_broadcast((P, LH, LD)), ALU.mult)
                            V.tensor_tensor(rot2[s][:, q].rearrange("p h (b d) -> p h b d", b=2),
                                            got.rearrange("p (h b d) -> p h b d", h=LH, b=2)[:, :, ::-1],
                                            factor[1].rearrange("p o (b d) -> p o b d", b=2).to_broadcast((P, LH, 2, LD // 2)),
                                            ALU.mult).then_inc(drain(s, (l, key)), 1)
                        link(s, V.tensor_reduce(rs[s][:, 0], sq[s].rearrange("p q h d -> p (q h) d"), AX.X, ALU.add))
                        link(s, V.tensor_scalar(rs[s][:, 0], rs[s][:, 0], 1e-24, None, ALU.max))
                        rsqrt(s, 2 * LH)
                        V.tensor_scalar(rs[s][:, 3, 0:LH], rs[s][:, 1, 0:LH], 8.0, None, ALU.mult).then_inc(knorm_ready[s], 1)
                        wait_drained(dve, s, n, (l, "q"))
                        V.tensor_tensor(qk[s][:, 0].rearrange("p a t -> p (a t)"), rot1[s][:, 0].rearrange("p h d -> p (h d)"),
                                        rot2[s][:, 0].rearrange("p h d -> p (h d)"), ALU.add).then_inc(q_ready[s], 1)

                    def rowmax(s, l, p):
                        key = (l, f"sim{p}")
                        wait_filled(dve, s, n, key)
                        if p == 0:
                            dve.wait_ge(knorm_ready[s], n * DEPTH + (l + 1))
                        h0, h1 = heads_of(p)
                        heads = slice(h0, h1 + 1, 2)
                        link(s, V.tensor_reduce(mx[s][:, 0, heads], held(s, key)[:].rearrange("p (e t) -> p e t", e=2),
                                                AX.X, ALU.max))
                        V.scalar_tensor_tensor(out=mx[s][:, 1, heads], in0=mx[s][:, 0, heads], scalar=-1.0,
                                               in1=rs[s][:, 3, heads], op0=ALU.mult, op1=ALU.mult).then_inc(negmax_ready[s], 1)

                    def turned_p(s, l, p):
                        key = (l, f"p{p}")
                        wait_filled(dve, s, n, key)
                        V.tensor_copy(pT[s][:, p % 2].rearrange("p a t -> p (a t)"), held(s, key)[:]).then_inc(drain(s, key), 1)

                    def divide(s, l, half):
                        key = (l, f"o{half}")
                        wait_filled(dve, s, n, key)
                        o = held(s, key)[:, 0:4 * LV].rearrange("p (h d) -> p h d", h=4)
                        link(s, V.reciprocal(rd[s][:, 0, 0:4].unsqueeze(2), o[:, :, LD:LV]))
                        V.tensor_tensor(on[s].rearrange("p c t -> p (c t)")[:, half * 4 * LD:(half + 1) * 4 * LD].rearrange("p (h d) -> p h d", h=4),
                                        o[:, :, 0:LD], rd[s][:, 0, 0:4].unsqueeze(2).to_broadcast((P, 4, LD)),
                                        ALU.mult).then_inc(drain(s, key), 1)

                    def add_attention(s, l):
                        wait_filled(dve, s, n, (l, "wo"))
                        V.tensor_tensor(xl[s][:], xl[s][:], held(s, (l, "wo"))[:, 0:D], ALU.add).then_inc(drain(s, (l, "wo")), 1)

                    def norm(s, l):
                        wait_drained(dve, s, n, (l, "wo"))
                        dve.wait_ge(tail_read[s], n * (16 * DEPTH) + 16 * (l + 1))
                        dve.wait_ge(shifted[s], n * (16 * DEPTH) + 16 * (l + 1))
                        normalise(s, [xl[s][:, 0:P], xs2[s][:]]).then_inc(z_ready[s], 1)

                    def gates(s, l):
                        for m in range(HC):
                            key = (l, f"ag{m // 2}")
                            rows = LAST if m == HC - 1 else P
                            b = (l * 2) * HC + m
                            if m % 2 == 1:
                                dve.wait_ge(gelu_ready[s], n * (HC * DEPTH) + (l * HC + m + 1))
                                for k in (m - 1, m):
                                    rows = LAST if k == HC - 1 else P
                                    b = (l * 2) * HC + k
                                    at = 2 * (k % 2) * P
                                    ins = V.scalar_tensor_tensor(out=hid[s][0:rows, k], in0=held(s, key)[0:rows, at:at + P],
                                                                 scalar=B1[0:rows, b:b + 1], in1=gl[s][0:rows, k],
                                                                 op0=ALU.add, op1=ALU.mult)
                                ins.then_inc(drain(s, key), 1)

                    def add_ffn(s, l):
                        wait_filled(dve, s, n, (l, "w2"))
                        dve.wait_ge(xb_ready[s], n * DEPTH + (l + 1))
                        dve.wait_ge(tail_saved[s], n * (16 * DEPTH) + 16 * (l + 1))
                        V.tensor_tensor(xl[s][:], xb[s][:], held(s, (l, "w2"))[:, 0:D], ALU.add).then_inc(drain(s, (l, "w2")), 1)

                    def finish(s):
                        wait_drained(dve, s, n, (DEPTH - 1, "w2"))
                        dve.wait_ge(y_stored[s], n * 16)
                        link(s, V.tensor_tensor(y[s][:], xl[s][:], mod[s][:, 3 * D:], ALU.mult))
                        V.tensor_tensor(y[s][:], y[s][:], x1[s][:], ALU.add).then_inc(y_ready[s], 1)

                    for step in (a_norm, a_bias, a_phi, a_mask, a_divide, a_add, modulate):
                        for s in range(STREAMS):
                            step(s)
                    for l in range(DEPTH):
                        for s in range(STREAMS):
                            rotate(s, l)
                        for s in range(STREAMS):
                            rowmax(s, l, 0)
                            rowmax(s, l, 1)
                        for p in range(PAIRS):
                            for s in range(STREAMS):
                                if p % 2 == 0:
                                    turned_p(s, l, p)
                                if p + 2 < PAIRS:
                                    rowmax(s, l, p + 2)
                                if p == 2:
                                    divide(s, l, 0)
                        for s in range(STREAMS):
                            divide(s, l, 1)
                        for step in (add_attention, norm, gates, add_ffn):
                            for s in range(STREAMS):
                                step(s, l)
                    for s in range(STREAMS):
                        finish(s)
                    assert links == [CHAIN] * STREAMS, links

        @block.gpsimd
        def _(pool):
            G = nc.gpsimd
            pool.wait_ge(consts_ready, NCONST)
            pool.wait_ge(rotary_loaded, 16 * DEPTH)
            pool.wait_ge(weights_loaded, 16 * WEIGHT_LOADS)
            for l in range(DEPTH):
                for q in range(2):
                    for f in range(2):
                        fac = ROT[:, l, :, q, f].rearrange("p t (b d) -> p t b d", b=2)
                        sc = scales[:, l, q].rearrange("p (b d) -> p b d", b=2)
                        if f == 1:
                            sc = sc[:, ::-1]
                        G.tensor_tensor(fac, fac, sc.unsqueeze(1).to_broadcast((P, TILES, 2, LD // 2)), ALU.mult).then_inc(factors_ready, 1)
            with pool.Fori(0, ROUNDS) as j:
                with pool.Fori(0, TILES) as i:
                    n = j * TILES + i
                    for l in range(DEPTH):
                        for s in range(STREAMS):
                            wait_drained(pool, s, n, (l, "k"))
                            k = qk[s][:, 1].rearrange("p a t -> p (a t)")
                            G.tensor_tensor(k, rot1[s][:, 1].rearrange("p h d -> p (h d)"), rot2[s][:, 1].rearrange("p h d -> p (h d)"),
                                            ALU.add).then_inc(ksum_ready[s], 1)
                            pool.wait_ge(ksum_ready[s], n * DEPTH + (l + 1))
                            pool.wait_ge(knorm_ready[s], n * DEPTH + (l + 1))
                            k = k.rearrange("p (h d) -> p h d", h=LH)
                            G.tensor_tensor(k, k, rs[s][:, 1, LH:2 * LH].unsqueeze(2).to_broadcast((P, LH, LD)), ALU.mult).then_inc(k_ready[s], 1)
                        for s in range(STREAMS):
                            wait_filled(pool, s, n, (l, "o1"))
                            G.tensor_tensor(kprev[s][:, l], kT[s][:], ZERO[:].unsqueeze(2).to_broadcast((P, PAIRS, P)),
                                            ALU.add).then_inc(kv_moved[s], 1)
                            G.tensor_scalar(vprev[s][:, l], vw[s][:], 1.0, 0.0, ALU.mult, ALU.add).then_inc(kv_moved[s], 1)
                        for s in range(STREAMS):
                            wait_drained(pool, s, n, (l, "wo"))
                            G.tensor_tensor(xb[s][:], xl[s][:], B2[:, l * D:(l + 1) * D], ALU.add).then_inc(xb_ready[s], 1)


def kernel(**inputs):
    import concourse.bacc as bacc
    from concourse.bass_utils import run_bass_kernel_spmd

    def of(name):
        return np.ascontiguousarray(inputs[name])

    x = of("L0_attn_x")
    B, N, _ = x.shape
    R, T = B // STREAMS, N // P
    xt = x.reshape(R, STREAMS, T, P, D).transpose(1, 0, 2, 3, 4).reshape(STREAMS, R * T, P, D)
    xt = np.concatenate([xt, np.zeros((STREAMS, 1, P, D), x.dtype)], axis=1)

    f4 = np.float32
    half = np.arange(0, LD, 2, dtype=f4)
    inv_freq = (f4(1.0) / np.power(f4(10000.0), half / f4(LD))).astype(f4)
    t = np.arange(N, dtype=f4)
    freqs = (t[:, None] * inv_freq[None, :]).astype(f4).astype(np.float64)
    base = ((half + f4(0.4 * LD)) / f4(1.4 * LD)).astype(np.float64)
    power = (t.astype(np.float64) - N // 2) / float(WINDOW // 2)
    scale = base[None, :] ** power[:, None]
    cos, sin = np.cos(freqs), np.sin(freqs)
    rot = np.empty((N, 2, 2, LD), f4)
    for q, sc in enumerate((scale, 1.0 / scale)):
        rot[:, q, 0] = np.concatenate([cos * sc, cos * sc], axis=1)
        rot[:, q, 1] = np.concatenate([-sin * sc, sin * sc], axis=1)
    rot = rot.reshape(T, P, 2 * 2 * LD).transpose(1, 0, 2).reshape(P, T * 4 * LD)

    r = np.arange(P)
    blockdiag = np.zeros((P, AC, AG, AV), f4)
    for g in range(AG):
        blockdiag[g * PAD:g * PAD + AD, :, g] = 1.0
    prev = np.where(r[None, :] >= r[:, None], 0.0, MASKED)
    this = np.where(r[None, :] <= r[:, None], 0.0, MASKED)
    window = np.empty((P, 2, 2, 2, WINDOW), f4)
    window[:, 0, :, 0] = MASKED
    window[:, 1, :, 0] = prev[:, None, :]
    window[:, :, :, 1] = this[:, None, None, :]

    def columns(v, chunks):
        return v.reshape(v.shape[0], v.shape[1], chunks, P).transpose(3, 0, 1, 2).reshape(P, -1)

    b1 = np.zeros((DEPTH, 2, HC * P), f4)
    b1[:, :, 0:HID] = of("L0_ffn_b1").reshape(DEPTH, 2, HID)
    arrays = {
        "x": xt,
        "waT": np.concatenate([of(f"L0_attn_W{k}").T for k in "qkv"], axis=1),
        "woaT": of("L0_attn_Wo").T,
        "ba": np.concatenate([of(f"L0_attn_b{k}") for k in "qkv"])[None],
        "bo": of("L0_attn_bo")[None],
        "wqkv": of("L0_ffn_wqkv"), "qs": of("L0_ffn_q_scale"), "ks": of("L0_ffn_k_scale"), "wo": of("L0_ffn_wo"),
        "ln_g": columns(np.stack([of("L0_ffn_ln_g"), of("L0_ffn_ln_b")], axis=1), KC), "ln_b": of("L0_ffn_ln_b"),
        "w1": of("L0_ffn_w1"), "b1": columns(b1, HC), "w2": of("L0_ffn_w2"), "b2": of("L0_ffn_b2").reshape(1, -1),
        "cT": of("L0_c").T, "wmod": of("L0_wmod"),
        "rotary": rot, "ident": np.eye(P, dtype=f4), "causal": (r[:, None] <= r[None, :]).astype(f4),
        "blockdiag": blockdiag.reshape(P, -1), "window": window.reshape(P, -1),
    }
    arrays = {f"in_{k}": np.ascontiguousarray(v) for k, v in arrays.items()}

    nc = bacc.Bacc("TRN2", target_bir_lowering=False, num_devices=1)
    args = [nc.dram_tensor(k, v.shape, mybir.dt.from_np(v.dtype), kind="ExternalInput").ap() for k, v in arrays.items()]
    out = nc.dram_tensor("out_x", (STREAMS, R * T, P, D), F32, kind="ExternalOutput").ap()
    adaln_block(nc, *args, out)
    got = run_bass_kernel_spmd(nc, [arrays], core_ids=[0]).results[0]["out_x"]
    return got.reshape(STREAMS, R, T, P, D).transpose(1, 0, 2, 3, 4).reshape(B, N, D)
```

```python
from contextlib import ExitStack
from functools import partial

import numpy as np

import concourse.bass as bass
from concourse import mybir

F32 = mybir.dt.float32
BF16 = mybir.dt.bfloat16
I32 = mybir.dt.int32
ALU = mybir.AluOpType
ACT = mybir.ActivationFunctionType
AX = mybir.AxisListType

P = 128
D = 256
KC = D // P
STREAMS = 2
AH, AD = 16, 16
AG = P // AD
QUARTERS = 4
AV = AD + 1
DEPTH, LH, LD = 2, 8, 64
INNER = LH * LD
PAIRS = LH // 2
LV = LD + 1
HID = 682
HC = -(-HID // P)
LAST = HID - (HC - 1) * P
WINDOW = 128
MASKED = -1e30
EPS_LN, EPS_DEN = 1e-5, 1e-6
MAGIC = float(0x5F3759DF)

FILLS_A = [("z", 0), ("qk", 1), ("v", 2), ("phi", 3),
           ("score0", 1), ("score1", 0), ("score2", 3), ("score3", 1), ("num", 2), ("kv", 0),
           ("o", 3), ("wo", 1)]
FILLS_L = [("x", 1), ("k", 3), ("q", 2), ("v", 0), ("kT", 0), ("qT", 1),
           ("sim0", 1), ("sim1", 2), ("p0", 0), ("sim2", 1), ("p1", 0), ("sim3", 2), ("p2", 0), ("o0", 3),
           ("p3", 0), ("o1", 3), ("o", 0), ("wo", 1), ("z", 2), ("ag0", 3), ("ag1", 0), ("ag2", 1), ("w2", 2)]


def bank_turns():
    turn, count = {}, [0] * 4
    for key, bank in [(("A", k), b) for k, b in FILLS_A] + [((l, k), b) for l in range(DEPTH) for k, b in FILLS_L]:
        turn[key] = (bank, count[bank])
        count[bank] += 1
    return turn, count


TURN, FILLS = bank_turns()

STEPS_A = ["norm_a", "turn_z_a", "project_a", "turn_phi", "scores", "numerators", "turn_o_a", "out_a", "modulate"]
ATTEND_BESIDE_FFN = [
    (0, "turn_k"), (0, "turn_q"), (1, "norm"), (0, "sim0"), (0, "sim1"), (1, "turn_z"), (0, "exp0"), (0, "exp1"),
    (1, "widen0"), (0, "turn_p0"), (0, "sim2"), (0, "exp2"), (0, "turn_p1"), (0, "weigh0"), (1, "widen1"),
    (0, "sim3"), (0, "exp3"), (0, "turn_p2"), (0, "weigh1"), (1, "gelu0"), (1, "widen2"), (1, "gelu1"), (1, "gelu2"),
    (0, "turn_p3"), (0, "weigh2"), (1, "narrow"), (0, "weigh3"), (1, "turn_x"), (1, "project_k"), (0, "turn_o"),
    (1, "project_q"), (0, "project_o"), (1, "rotate_q"), (1, "project_v")]
TO_ATTENTION = ("turn_x", "project_k", "project_q", "project_v")


TO_LINEAR = {"widen1": "norm_a", "turn_x": "turn_z_a", "project_k": "project_a"}
ATTEND_BESIDE_LINEAR = [
    (0, "turn_x"), (1, "norm_a"), (0, "project_k"), (0, "project_q"), (0, "rotate_q"), (1, "turn_z_a"),
    (0, "project_v"), (1, "project_a"), (0, "turn_k"), (0, "turn_q"), (0, "sim0"), (0, "exp0"), (1, "turn_phi"),
    (0, "sim1"), (0, "exp1"), (0, "turn_p0"), (0, "sim2"), (0, "exp2"), (1, "scores"), (0, "turn_p1"), (0, "weigh0"),
    (0, "sim3"), (0, "exp3"), (1, "numerators"), (1, "turn_o_a"), (0, "turn_p2"), (0, "weigh1"), (1, "out_a"),
    (0, "turn_p3"), (0, "weigh2"), (0, "weigh3"), (1, "modulate"), (0, "turn_o"), (0, "project_o"), (1, "turn_x"),
    (1, "project_k"), (1, "project_q"), (1, "rotate_q"), (1, "project_v")]
LINEAR_BESIDE_FFN = [
    (0, "turn_phi"), (1, "norm"), (0, "scores"), (0, "numerators"), (1, "turn_z"), (0, "turn_o_a"), (1, "widen0"),
    (0, "out_a"), (1, "widen1"), (1, "gelu0"), (0, "modulate"), (1, "widen2"), (1, "gelu1"), (1, "gelu2"),
    (1, "narrow")]


def issue_order():
    order = [(s, step, 0) for s, step in ATTEND_BESIDE_LINEAR]
    for l in range(DEPTH):
        for a in range(STREAMS):
            if (a, l) == (0, 0):
                continue
            other, lo = 1 - a, l if a == 1 else l - 1
            for who, step in ATTEND_BESIDE_FFN:
                if who == 0:
                    order.append((a, step, l))
                elif step not in (*TO_ATTENTION, "rotate_q"):
                    order.append((other, step, lo))
                elif lo + 1 < DEPTH:
                    order.append((other, step, lo + 1))
                if who == 1 and (other, lo) == (0, DEPTH - 1) and step in TO_LINEAR:
                    order.append((0, TO_LINEAR[step], 0))
    return order + [(s, step, DEPTH - 1) for s, step in LINEAR_BESIDE_FFN]


ORDER = issue_order()
FIRST = [(0, step, 0) for step in STEPS_A]
CHAIN_FIRST, CHAIN = 25, 191


def adaln_block(nc, x, waT, woaT, ba, bo, wqkv, qs, ks, wo, ln_g, ln_b, w1, b1, w2, b2, cT, wmod,
                rotary, ident, causal, blockdiag, window, out):
    B = cT.shape[1]
    STREAM_TILES = out.shape[1]
    ROUNDS = B // STREAMS
    TILES = STREAM_TILES // ROUNDS

    mod_dram = nc.dram_tensor("mod_rows", (B + STREAMS, 6 * D), F32, kind="Internal").ap()

    with ExitStack() as ctx:
        def sb(name, shape, dt=F32):
            return ctx.enter_context(nc.sbuf_tensor(name, shape, dt))

        def sem(name):
            return ctx.enter_context(nc.semaphore(name))

        def each(make, name, *a):
            return [make(f"{name}_{s}", *a) for s in range(STREAMS)]

        WA = sb("WA", [P, KC, 3 * D])
        WOA = sb("WOA", [P, KC, D])
        WQKV = sb("WQKV", [P, DEPTH, KC, 3 * INNER])
        WO = sb("WO", [P, DEPTH, INNER // P, D])
        W1 = sb("W1", [P, DEPTH, KC, 2 * HID])
        W2 = sb("W2", [P, DEPTH, HC, D])
        BA = sb("BA", [P, 3 * D])
        BO = sb("BO", [P, D])
        B2 = sb("B2", [P, DEPTH * D])
        B1 = sb("B1", [P, DEPTH * 2 * HC])
        LN = sb("LN", [P, 2 * DEPTH * KC])
        ROT = sb("ROT", [P, DEPTH, TILES, 2, 2, LD])
        IDENT = sb("IDENT", [P, P])
        IDENTB = sb("IDENTB", [P, P], BF16)
        CAUSAL = sb("CAUSAL", [P, P])
        ZERO = sb("ZERO", [P, 1])
        BLOCKDIAG = sb("BLOCKDIAG", [P, AH * AV])
        WINDOWB = sb("WINDOWB", [P, 2, 2 * 2 * WINDOW], BF16)

        xin = each(sb, "xin", [P, D])
        x1 = each(sb, "x1", [P, D])
        xl = each(sb, "xl", [P, D])
        mod = each(sb, "mod", [P, 4 * D])
        modT = each(sb, "modT", [P, 2 * KC])
        state = each(sb, "state", [P, AH * AV])
        tailcol = each(sb, "tailcol", [P, DEPTH])
        tailrow = each(sb, "tailrow", [1, DEPTH, P])
        qT = each(sb, "qT", [P, 2, PAIRS, P])
        kprev = each(sb, "kprev", [P, DEPTH, PAIRS, P])
        vprev = each(sb, "vprev", [P, DEPTH, LH, LV])
        st = each(sb, "st", [P, 2, 6])
        mv = each(sb, "mv", [P, 2])
        RS = sb("RS", [P, 4, 4 * LH + 2])
        KCOL, QCOL, LNCOL = (0, 3 * LH + 2), (LH, 2 * LH + 2), (2 * LH + 1, 2 * LH)
        z = each(sb, "z", [P, D])
        zT = each(sb, "zT", [P, KC, P + 1])
        v1 = each(sb, "v1", [P, AH, AV])
        vw = each(sb, "vw", [P, LH, LV])
        mx = each(sb, "mx", [P, 2, LH])
        rd = each(sb, "rd", [P, 2, AH])
        xs2 = each(sb, "xs2", [P, P])
        spare = each(sb, "spare", [P, 1])
        y = each(sb, "y", [P, D])

        SCRATCH = 5632
        scratch = each(sb, "scratch", [P, SCRATCH])

        def carve(at, *shape):
            n = int(np.prod(shape))
            assert at + n <= SCRATCH
            names = " ".join("abcd"[:len(shape)])
            sizes = dict(zip("bcd", shape[1:]))
            return [t[:, at:at + n].rearrange(f"p ({names}) -> p {names}", **sizes) for t in scratch]

        qkb = carve(0, 2 * AH, AD)
        ex = carve(512, 2 * AH, AD)
        below = carve(1024, 2 * AH, AD)
        spreadq = carve(0, KC, AG, P)
        t0 = carve(0, AH * AV)
        branch = carve(512, D)
        phi = carve(2048, 2, D)
        phiT = carve(2560, 2, KC, P)
        sm = carve(3072, AH, P)
        oa = carve(5120, AH, AD)
        oaT = carve(5376, KC, P)
        sq = carve(0, 2, LH, LD)
        rot1 = carve(1024, 2, LH, LD)
        rot2 = carve(2048, 2, LH, LD)
        qk = carve(3072, 2, PAIRS, P)
        kT = carve(4608, PAIRS, P)
        pr = carve(0, 2, 4, WINDOW)
        pT = carve(1024, 2, 4, P)
        on = carve(2048, INNER // P, P)
        oT = carve(2560, INNER // P, P)
        gl = carve(0, HC, P)
        hid = carve(768, HC, P)
        xb = carve(1536, D)

        bank = [[ctx.enter_context(nc.psum_tensor(f"bank_{s}_{b}", [P, 512], F32)) for b in range(4)]
                for s in range(STREAMS)]

        filled = [[sem(f"filled_{s}_{b}") for b in range(4)] for s in range(STREAMS)]
        drained = [[sem(f"drained_{s}_{b}") for b in range(4)] for s in range(STREAMS)]
        modulation_loaded, weights_loaded, rotary_loaded = sem("modulation_loaded"), sem("weights_loaded"), sem("rotary_loaded")
        silu_ready, gate_step, modrow_full, modrow_ready, mod_stored = (
            sem("silu_ready"), sem("gate_step"), sem("modrow_full"), sem("modrow_ready"), sem("mod_stored"))
        consts_ready, factors_ready = sem("consts_ready"), sem("factors_ready")
        xin_loaded, mod_loaded, tails_zeroed, state_zeroed = (
            each(sem, "xin_loaded"), each(sem, "mod_loaded"), each(sem, "tails_zeroed"), each(sem, "state_zeroed"))
        spread_by_scalar, spread_by_vector = each(sem, "spread_by_scalar"), each(sem, "spread_by_vector")
        chain = sem("vector_chain")
        z_ready = each(sem, "z_ready")
        exp_ready, below_ready, phi_ready, state_ready, x1_ready, xl_ready, y_ready, y_stored = (
            each(sem, "exp_ready"), each(sem, "below_ready"), each(sem, "phi_ready"), each(sem, "state_ready"),
            each(sem, "x1_ready"), each(sem, "xl_ready"), each(sem, "y_ready"), each(sem, "y_stored"))
        squares_ready = each(sem, "squares_ready")
        q_ready, ksum_ready, knorm_ready, k_ready = (
            each(sem, "q_ready"), each(sem, "ksum_ready"), each(sem, "knorm_ready"), each(sem, "k_ready"))
        negmax_ready = each(sem, "negmax_ready")
        kv_moved = each(sem, "kv_moved")
        tail_read, tail_saved, shifted = each(sem, "tail_read"), each(sem, "tail_saved"), each(sem, "shifted")
        tail_used = each(sem, "tail_used")
        gelu_ready = each(sem, "gelu_ready")
        xb_ready = each(sem, "xb_ready")

        def held(s, key):
            return bank[s][TURN[key][0]]

        def wait_free(eng, s, n, key):
            b, turn = TURN[key]
            eng.wait_ge(drained[s][b], n[s] * FILLS[b] + (turn + AHEAD))

        def wait_filled(eng, s, n, key):
            b, turn = TURN[key]
            eng.wait_ge(filled[s][b], n[s] * FILLS[b] + (turn + 1))

        def wait_drained(eng, s, n, key):
            b, turn = TURN[key]
            eng.wait_ge(drained[s][b], n[s] * FILLS[b] + (turn + 1 + AHEAD))

        def fill(s, key):
            return filled[s][TURN[key][0]]

        def drain(s, key):
            return drained[s][TURN[key][0]]

        AHEAD = 1
        given_ahead = [*drained[0], *drained[1], *state_ready, *kv_moved, *tail_saved, *y_ready, *y_stored]

        WEIGHT_LOADS = 8 + 5 * DEPTH + 5
        NCONST = 12

        WM = [ROT[:, l].rearrange("p t q f d -> p (t q f d)")[:, 0:6 * D] for l in range(DEPTH)]
        crow = z[0][:, 0:KC * B]
        srow = z[1][:, 0:KC * B]
        modrow = scratch[0][0:B, 0:6 * D]
        modtmp = scratch[0][0:B, 6 * D:8 * D]
        scales = y[0][:, 0:DEPTH * 2 * LD].rearrange("p (l q d) -> p l q d", l=DEPTH, q=2)
        windowf = scratch[1][:, 0:2 * 4 * WINDOW]

        def own(eng, value, most):
            reg = eng.alloc_register(f"own_{nc.next_id()}")
            eng.reg_mov(reg, value)
            return eng.snap(reg, min_val=0, max_val=most)

        def run_passes(eng, one_pass, begin_batch=None):
            def place(j, i, last):
                n = j * TILES + i
                ns = [own(eng, n, STREAM_TILES - 1) for s in range(STREAMS)]
                iis = [i if last else own(eng, i, TILES - 1) for s in range(STREAMS)]
                return ORDER, ns, iis, [own(eng, n + 1, STREAM_TILES), ns[1]], [j + 1 if last else j, j], last

            one_pass(FIRST, [0, 0], [0, 0], [0, 0], [0, 0], True)
            with eng.Fori(0, ROUNDS) as j:
                if begin_batch:
                    begin_batch(j)
                with eng.Fori(0, TILES - 1) as i:
                    one_pass(*place(j, i, False))
                one_pass(*place(j, TILES - 1, True))

        def issue(order, steps):
            for s, step, l in order:
                if step in steps:
                    steps[step](s, l)

        block = ctx.enter_context(nc.Block())

        @block.sync
        def _(sp):
            count = [0]

            def load(dst, src):
                sp.dma_start(dst, src).then_inc(weights_loaded, 16)
                count[0] += 1

            sp.dma_start(crow.rearrange("p (c b) -> p c b", c=KC), cT.rearrange("(c p) b -> p c b", p=P)).then_inc(modulation_loaded, 16)
            for c in range(KC):
                sp.dma_start(WM[c], wmod[c * P:(c + 1) * P]).then_inc(modulation_loaded, 16)
            for s in range(STREAMS):
                sp.dma_start(xin[s][:], x[s, 0]).then_inc(xin_loaded[s], 16)
            load(IDENT[:], ident)
            load(WA[:], waT.rearrange("(c p) n -> p c n", p=P))
            load(BA[:], ba.partition_broadcast(P).rearrange("p o n -> p (o n)"))
            load(CAUSAL[:], causal)
            load(BLOCKDIAG[:], blockdiag)
            load(WOA[:], woaT.rearrange("(c p) n -> p c n", p=P))
            load(BO[:], bo.partition_broadcast(P).rearrange("p o n -> p (o n)"))
            load(windowf, window)
            for l in range(DEPTH):
                load(WQKV[:, l], wqkv[l].rearrange("(c p) n -> p c n", p=P))
                load(WO[:, l], wo[l].rearrange("(c p) n -> p c n", p=P))
                load(W1[:, l], w1[l].rearrange("(c p) n -> p c n", p=P))
                load(W2[:, l, 0:HC - 1], w2[l, 0:(HC - 1) * P].rearrange("(c p) n -> p c n", p=P))
                load(W2[0:LAST, l, HC - 1], w2[l, (HC - 1) * P:HID])
            load(B2[:], b2.partition_broadcast(P).rearrange("p o n -> p (o n)"))
            load(B1[:], b1)
            load(LN[:], ln_g)
            load(scales[:, :, 0], qs.partition_broadcast(P))
            load(scales[:, :, 1], ks.partition_broadcast(P))
            assert count[0] == WEIGHT_LOADS
            sp.wait_ge(modrow_full, 3)
            for l in range(DEPTH):
                sp.dma_start(ROT[:, l].rearrange("p t q f d -> p (t q f d)"), rotary).then_inc(rotary_loaded, 16)
            sp.wait_ge(modrow_ready, 6)
            sp.dma_start(mod_dram[0:B], modrow).then_inc(mod_stored, 16)
            sp.dma_start(mod_dram[B:B + STREAMS], modrow[0:STREAMS]).then_inc(mod_stored, 16)

            def one_pass(order, n, i, na, ja, next_batch):

                def prefetch(s, l):
                    sp.wait_ge(x1_ready[s], na[s] + 1)
                    sp.dma_start(xin[s][:], x[s, bass.ds(na[s] + 1, 1)].rearrange("o p d -> (o p) d")).then_inc(xin_loaded[s], 16)

                def last_token(s, l):
                    if l == 0:
                        sp.wait_ge(tails_zeroed[s], ja[1] + 1)
                        sp.wait_ge(tail_saved[s], ja[1] * (TILES * 16 * DEPTH) + (i[s] * (16 * DEPTH) + AHEAD))
                        sp.wait_ge(z_ready[s], n[s] * 3 + 1)
                    else:
                        sp.wait_ge(z_ready[s], n[s] * 3 + (1 + l))
                    sp.dma_start(xs2[s][0:1, :], tailrow[s][:, l]).then_inc(tail_read[s], 16)

                def shift_tokens(s, l):
                    wait_drained(sp, s, n, (l, "wo"))
                    sp.dma_start(xs2[s][1:P, :], xl[s][0:P - 1, P:D]).then_inc(shifted[s], 16)
                    sp.wait_ge(tail_read[s], n[s] * (16 * DEPTH) + 16 * (l + 1))
                    sp.dma_start(tailrow[s][:, l], xl[s][P - 1:P, P:D]).then_inc(tail_saved[s], 16)

                def store(s, l):
                    if l == DEPTH - 1:
                        sp.wait_ge(y_ready[s], n[s] + (1 + AHEAD))
                        sp.dma_start(out[s, bass.ds(n[s], 1)].rearrange("o p d -> (o p) d"), y[s][:]).then_inc(y_stored[s], 16)

                issue(order, {"out_a": prefetch, "turn_q": last_token, "project_o": shift_tokens, "narrow": store})

            run_passes(sp, one_pass)
            for s in range(STREAMS):
                sp.wait_ge(y_stored[s], 16 * STREAM_TILES + AHEAD)
                sp.wait_ge(xin_loaded[s], 16 * (STREAM_TILES + (2 if s == 0 else 1)))
                sp.wait_ge(tail_saved[s], 16 * DEPTH * STREAM_TILES + AHEAD)

        @block.tensor
        def _(pe):
            def project(s, n, key, lhsT, rhs, cols, rows=P):
                wait_free(pe, s, n, key)
                for c in range(len(lhsT)):
                    mm = nc.tensor.matmul(held(s, key)[0:rows, 0:cols], lhsT[c], rhs[c],
                                          start=(c == 0), stop=(c == len(lhsT) - 1))
                mm.then_inc(fill(s, key), 1)

            def turn(s, n, key, blocks):
                wait_free(pe, s, n, key)
                for k, b in enumerate(blocks):
                    mm = nc.tensor.transpose(held(s, key)[:, k * P:(k + 1) * P], b, IDENT[:])
                mm.then_inc(fill(s, key), 1)

            def halves(t):
                return [t[:, c * P:(c + 1) * P] for c in range(KC)]

            pe.wait_ge(modulation_loaded, 48)
            pe.wait_ge(silu_ready, 1)
            for k in range(3):
                for c in range(KC):
                    mm = nc.tensor.matmul(bank[0][k][0:B, :], srow[:, c * B:(c + 1) * B], WM[c][:, k * 512:(k + 1) * 512],
                                          start=(c == 0), stop=(c == KC - 1))
                mm.then_inc(modrow_full, 1)
            pe.wait_ge(weights_loaded, 16 * WEIGHT_LOADS)
            pe.wait_ge(consts_ready, NCONST)
            pe.wait_ge(modrow_ready, 6)

            def one_pass(order, n, i, na, ja, next_batch):

                def a_turn_z(s, l):
                    pe.wait_ge(z_ready[s], na[s] * 3 + 1)
                    turn(s, na, ("A", "z"), halves(z[s]))

                def a_project(s, l):
                    wait_drained(pe, s, na, ("A", "z"))
                    h = [zT[s][:, c, 0:P] for c in range(KC)]
                    project(s, na, ("A", "qk"), h, [WA[:, c, 0:2 * D] for c in range(KC)], 2 * D)
                    project(s, na, ("A", "v"), h, [WA[:, c, 2 * D:] for c in range(KC)], D)

                def a_turn_phi(s, l):
                    pe.wait_ge(phi_ready[s], na[s] + 1)
                    turn(s, na, ("A", "phi"), [phi[s][:, q, c * P:(c + 1) * P] for q in range(2) for c in range(KC)])

                def a_scores(s, l):
                    wait_drained(pe, s, na, ("A", "phi"))
                    for m in range(QUARTERS):
                        key = ("A", f"score{m}")
                        wait_free(pe, s, na, key)
                        c, g = m // 2, m % 2 * (AG // 2)
                        if c == 0:
                            for who in (spread_by_scalar, spread_by_vector):
                                pe.wait_ge(who[s], na[s] * 2 + (m % 2 + 1))
                        nc.tensor.matmul(held(s, key)[:], phiT[s][:, 1, c], spreadq[s][:, c, g:g + AG // 2].rearrange("p g t -> p (g t)"),
                                         start=True, stop=True).then_inc(fill(s, key), 1)

                def a_numerators(s, l):
                    key = ("A", "num")
                    wait_free(pe, s, na, key)
                    pe.wait_ge(state_ready[s], na[s] + AHEAD)
                    pe.wait_ge(state_zeroed[s], ja[s] + 1)
                    acc = held(s, key)
                    w = AG * AV
                    for c in range(KC):
                        nc.tensor.matmul(acc[:, c * w:(c + 1) * w], phiT[s][:, 0, c], state[s][:, c * w:(c + 1) * w],
                                         start=(c == 0), stop=False, skip_group_check=True)
                    wait_drained(pe, s, na, ("A", "v"))
                    for h in range(AH):
                        if h % (AH // QUARTERS) == 0:
                            wait_drained(pe, s, na, ("A", f"score{h // (AH // QUARTERS)}"))
                        mm = nc.tensor.matmul(acc[:, h * AV:(h + 1) * AV], sm[s][:, h], v1[s][:, h],
                                              start=False, stop=(h == AH - 1), skip_group_check=True)
                    mm.then_inc(fill(s, key), 1)
                    key = ("A", "kv")
                    wait_free(pe, s, na, key)
                    for c in range(KC):
                        mm = nc.tensor.matmul(held(s, key)[:, c * w:(c + 1) * w], phi[s][:, 1, c * P:(c + 1) * P],
                                              v1[s][:, c * AG:(c + 1) * AG].rearrange("p h d -> p (h d)"), start=True, stop=True)
                    mm.then_inc(fill(s, key), 1)

                def a_turn_o(s, l):
                    wait_drained(pe, s, na, ("A", "num"))
                    flat = oa[s].rearrange("p h d -> p (h d)")
                    turn(s, na, ("A", "o"), halves(flat))

                def a_out(s, l):
                    wait_drained(pe, s, na, ("A", "o"))
                    project(s, na, ("A", "wo"), [oaT[s][:, c] for c in range(KC)], [WOA[:, c] for c in range(KC)], D)

                def turn_x(s, l):
                    if l == 0:
                        pe.wait_ge(xl_ready[s], n[s] + 1)
                    else:
                        wait_drained(pe, s, n, (l - 1, "w2"))
                    turn(s, n, (l, "x"), halves(xl[s]))

                def project_qkv(key, s, l):
                    wait_drained(pe, s, n, (l, "x"))
                    xs = [zT[s][:, c, 0:P] for c in range(KC)]
                    k = "qkv".index(key)
                    project(s, n, (l, key), xs, [WQKV[:, l, c, k * INNER:(k + 1) * INNER] for c in range(KC)], INNER)

                def turn_q(s, l):
                    pe.wait_ge(q_ready[s], n[s] * DEPTH + (l + 1))
                    turn(s, n, (l, "qT"), [qk[s][:, 0, p] for p in range(PAIRS)])

                def turn_k(s, l):
                    pe.wait_ge(k_ready[s], n[s] * DEPTH + (l + 1))
                    turn(s, n, (l, "kT"), [qk[s][:, 1, p] for p in range(PAIRS)])

                def sim(p, s, l):
                    if p == 0:
                        pe.wait_ge(kv_moved[s], n[s] * (2 * DEPTH) + (2 * l + AHEAD))
                    key = (l, f"sim{p}")
                    wait_free(pe, s, n, key)
                    first = (i[s] + (TILES - 1)) // TILES
                    nc.tensor.matmul(held(s, key)[:], IDENTB[:], WINDOWB[:, bass.ds(first, 1)].rearrange("p o n -> p (o n)"),
                                     start=True, stop=False, skip_group_check=True)
                    for e in range(2):
                        for kb, keys in enumerate((kprev[s][:, l, p], kT[s][:, p])):
                            col = (2 * e + kb) * WINDOW
                            mm = nc.tensor.matmul(held(s, key)[:, col:col + WINDOW], qT[s][:, e, p], keys,
                                                  start=False, stop=(e == 1 and kb == 1), skip_group_check=True)
                    mm.then_inc(fill(s, key), 1)

                def turn_p(p, s, l):
                    wait_drained(pe, s, n, (l, f"sim{p}"))
                    turn(s, n, (l, f"p{p}"), [pr[s][:, p % 2, k] for k in range(4)])

                def weigh_v(p, s, l):
                    key = (l, f"o{p // 2}")
                    if p % 2 == 0:
                        wait_free(pe, s, n, key)
                    wait_drained(pe, s, n, (l, f"p{p}"))
                    for e in range(2):
                        h = 2 * p + e
                        col = (h % 4) * LV
                        for kb, values in enumerate((vprev[s][:, l, h], vw[s][:, h])):
                            mm = nc.tensor.matmul(held(s, key)[:, col:col + LV], pT[s][:, p % 2, 2 * e + kb], values,
                                                  start=(p % 2 == 0 and e == 0 and kb == 0),
                                                  stop=(p % 2 == 1 and e == 1 and kb == 1), skip_group_check=True)
                    if p % 2 == 1:
                        mm.then_inc(fill(s, key), 1)

                def turn_o(s, l):
                    wait_drained(pe, s, n, (l, "o1"))
                    turn(s, n, (l, "o"), [on[s][:, c] for c in range(INNER // P)])

                def project_o(s, l):
                    wait_drained(pe, s, n, (l, "o"))
                    project(s, n, (l, "wo"), [oT[s][:, c] for c in range(INNER // P)], [WO[:, l, c] for c in range(INNER // P)], D)

                def turn_z(s, l):
                    pe.wait_ge(z_ready[s], n[s] * 3 + (2 + l))
                    turn(s, n, (l, "z"), halves(z[s]))

                def widen(m, s, l):
                    wait_drained(pe, s, n, (l, "z"))
                    key = (l, f"ag{m}")
                    wait_free(pe, s, n, key)
                    for k in range(2):
                        rows = LAST if 2 * m + k == HC - 1 else P
                        for g in range(2):
                            at = g * HID + (2 * m + k) * P
                            for c in range(KC):
                                mm = nc.tensor.matmul(held(s, key)[0:rows, (2 * k + g) * P:(2 * k + g + 1) * P],
                                                      W1[:, l, c, at:at + rows], zT[s][:, c, 0:P],
                                                      start=(c == 0), stop=(c == KC - 1))
                    mm.then_inc(fill(s, key), 1)

                def narrow(s, l):
                    key = (l, "w2")
                    wait_free(pe, s, n, key)
                    for m in range(HC):
                        if m % 2 == 0:
                            wait_drained(pe, s, n, (l, f"ag{m // 2}"))
                        rows = LAST if m == HC - 1 else P
                        mm = nc.tensor.matmul(held(s, key)[:, 0:D], hid[s][0:rows, m], W2[0:rows, l, m],
                                              start=(m == 0), stop=(m == HC - 1))
                    mm.then_inc(fill(s, key), 1)

                steps = {"turn_z_a": a_turn_z, "project_a": a_project, "turn_phi": a_turn_phi, "scores": a_scores,
                         "numerators": a_numerators, "turn_o_a": a_turn_o, "out_a": a_out,
                         "turn_x": turn_x, "turn_q": turn_q, "turn_k": turn_k, "turn_o": turn_o,
                         "project_o": project_o, "turn_z": turn_z, "narrow": narrow}
                steps.update({f"project_{k}": partial(project_qkv, k) for k in "qkv"})
                for p in range(PAIRS):
                    steps.update({f"sim{p}": partial(sim, p), f"turn_p{p}": partial(turn_p, p), f"weigh{p}": partial(weigh_v, p)})
                steps.update({f"widen{m}": partial(widen, m) for m in range(HC // 2)})
                issue(order, steps)

            run_passes(pe, one_pass)
        @block.scalar
        def _(act):
            act.wait_ge(modulation_loaded, 48)
            nc.scalar.activation(srow, crow, ACT.Silu).then_inc(silu_ready, 1)
            act.wait_ge(weights_loaded, 16 * WEIGHT_LOADS)
            act.wait_ge(consts_ready, NCONST)
            act.wait_ge(mod_stored, 32)

            def copy(dst, src):
                return nc.scalar.activation(dst, src, ACT.Copy)

            def load_modulation(s, j):
                act.wait_ge(y_ready[s], j * TILES + AHEAD)
                row = mod_dram[bass.ds(j * STREAMS + s, 1)]
                act.dma_start(mod[s][:], row[:, 2 * D:].partition_broadcast(P).rearrange("p o d -> p (o d)")).then_inc(mod_loaded[s], 16)
                with nc.allow_non_contiguous_dma(reason="two rows of 256 for each batch element, one to a partition"):
                    act.dma_start(modT[s][:], row[:, 0:2 * D].rearrange("o (r p) -> p (o r)", p=P)).then_inc(mod_loaded[s], 16)

            def begin_batch(j):
                load_modulation(1, j)
                for s in range(STREAMS):
                    act.wait_ge(tails_zeroed[s], j + 1)

            def one_pass(order, n, i, na, ja, next_batch):

                def affine_z(s, n, key, scale, bias):
                    wait_filled(act, s, n, key)
                    for c in range(KC):
                        ins = nc.scalar.activation(zT[s][:, c, 0:P], held(s, key)[:, c * P:(c + 1) * P], ACT.Identity,
                                                   scale=scale[c], bias=bias[c])
                    ins.then_inc(drain(s, key), 1)

                def a_h(s, l):
                    if s == 0 and next_batch:
                        load_modulation(s, ja[s])
                    act.wait_ge(mod_loaded[s], ja[s] * 32 + 32)
                    affine_z(s, na, ("A", "z"), [modT[s][:, KC + c:KC + c + 1] for c in range(KC)],
                             [modT[s][:, c:c + 1] for c in range(KC)])

                def a_exp(s, l):
                    act.wait_ge(below_ready[s], na[s] + 1)
                    nc.scalar.activation(ex[s][:], below[s][:], ACT.Exp).then_inc(exp_ready[s], 1)

                def a_phiT(s, l):
                    key = ("A", "phi")
                    wait_filled(act, s, na, key)
                    copy(phiT[s].rearrange("p q c t -> p (q c t)"), held(s, key)[:]).then_inc(drain(s, key), 1)
                    wait_drained(act, s, na, key)
                    for g in range(0, AG, 2):
                        ins = nc.scalar.activation(spreadq[s][:, :, g], phiT[s][:, 0], ACT.Copy, scale=BLOCKDIAG[:, g * AV:g * AV + 1])
                        if g % (AG // 2) == AG // 2 - 2:
                            ins.then_inc(spread_by_scalar[s], 1)

                def a_oT(s, l):
                    wait_filled(act, s, na, ("A", "o"))
                    copy(oaT[s].rearrange("p c t -> p (c t)"), held(s, ("A", "o"))[:, 0:D]).then_inc(drain(s, ("A", "o")), 1)

                def shift_x(s, l):
                    key = (l, "x")
                    wait_filled(act, s, n, key)
                    copy(zT[s][:, 1, 0:1], tailcol[s][:, l:l + 1]).then_inc(tail_used[s], 1)
                    copy(zT[s][:, 0, 0:P], held(s, key)[:, 0:P])
                    copy(zT[s][:, 1, 1:P + 1], held(s, key)[:, P:2 * P])
                    act.wait_ge(tail_used[s], n[s] * DEPTH + (l + 1))
                    copy(tailcol[s][:, l:l + 1], held(s, key)[:, 2 * P - 1:2 * P]).then_inc(drain(s, key), 1)

                def squares(q, s, l):
                    key = (l, "qk"[q])
                    wait_filled(act, s, n, key)
                    nc.scalar.activation(sq[s][:, q].rearrange("p h d -> p (h d)"), held(s, key)[:],
                                         ACT.Square).then_inc(squares_ready[s], 1)

                def keep_v(s, l):
                    wait_filled(act, s, n, (l, "v"))
                    act.wait_ge(kv_moved[s], n[s] * (2 * DEPTH) + (2 * l + AHEAD))
                    copy(vw[s][:, :, 0:LD], held(s, (l, "v"))[:].rearrange("p (h d) -> p h d", h=LH)).then_inc(drain(s, (l, "v")), 1)

                def turned(name, s, l):
                    dst = {"kT": kT, "o": oT}[name]
                    wait_filled(act, s, n, (l, name))
                    copy(dst[s].rearrange("p a t -> p (a t)"), held(s, (l, name))[:]).then_inc(drain(s, (l, name)), 1)

                def turned_q(s, l):
                    wait_filled(act, s, n, (l, "qT"))
                    for e in range(2):
                        rows = slice(e * LD, (e + 1) * LD)
                        ins = copy(qT[s][rows, e].rearrange("p a t -> p (a t)"), held(s, (l, "qT"))[rows])
                    ins.then_inc(drain(s, (l, "qT")), 1)

                def probs(p, s, l):
                    key = (l, f"sim{p}")
                    act.wait_ge(negmax_ready[s], n[s] * (PAIRS * DEPTH) + (PAIRS * l + p + 1))
                    for e in range(2):
                        h = 2 * p + e
                        ins = nc.scalar.activation(pr[s][:, p % 2, 2 * e:2 * e + 2].rearrange("p a t -> p (a t)"),
                                                   held(s, key)[:, e * 2 * WINDOW:(e + 1) * 2 * WINDOW], ACT.Exp,
                                                   scale=RS[:, 3, QCOL[s] + h:QCOL[s] + h + 1], bias=mx[s][:, 1, h:h + 1])
                    ins.then_inc(drain(s, key), 1)

                def turned_p(p, s, l):
                    key = (l, f"p{p}")
                    wait_filled(act, s, n, key)
                    copy(pT[s][:, p % 2].rearrange("p a t -> p (a t)"), held(s, key)[:]).then_inc(drain(s, key), 1)

                def affine(s, l):
                    g = (l * 2) * KC
                    affine_z(s, n, (l, "z"), [LN[:, g + c:g + c + 1] for c in range(KC)],
                             [LN[:, g + KC + c:g + KC + c + 1] for c in range(KC)])

                def gelus(pair, s, l):
                    for m in (2 * pair, 2 * pair + 1):
                        key = (l, f"ag{m // 2}")
                        if m % 2 == 0:
                            wait_filled(act, s, n, key)
                        rows = LAST if m == HC - 1 else P
                        b = (l * 2 + 1) * HC + m
                        at = (2 * (m % 2) + 1) * P
                        nc.scalar.activation(gl[s][0:rows, m], held(s, key)[0:rows, at:at + P], ACT.Gelu,
                                             bias=B1[0:rows, b:b + 1]).then_inc(gelu_ready[s], 1)

                steps = {"turn_z_a": a_h, "project_a": a_exp, "turn_phi": a_phiT, "turn_o_a": a_oT,
                         "turn_x": shift_x, "project_q": partial(squares, 0), "project_k": partial(squares, 1),
                         "project_v": keep_v, "turn_q": turned_q, "turn_k": partial(turned, "kT"),
                         "turn_o": partial(turned, "o"), "turn_z": affine}
                steps.update({f"exp{p}": partial(probs, p) for p in range(PAIRS)})
                steps.update({f"turn_p{p}": partial(turned_p, p) for p in range(PAIRS // 2)})
                steps.update({f"gelu{m}": partial(gelus, m) for m in range(HC // 2)})
                issue(order, steps)

            run_passes(act, one_pass, begin_batch)
        @block.vector
        def _(dve):
            V = nc.vector

            V.memset(ZERO[:], 0.0).then_inc(consts_ready, 1)
            for k, ahead in enumerate(given_ahead):
                V.memset(RS[:, 0, k:k + 1], 0.0).then_inc(ahead, AHEAD)
            for s in range(STREAMS):
                V.memset(kprev[s][:], 0.0).then_inc(consts_ready, 1)
                V.memset(vprev[s][:], 0.0).then_inc(consts_ready, 1)
                V.memset(v1[s][:], 1.0).then_inc(consts_ready, 1)
                V.memset(vw[s][:], 1.0).then_inc(consts_ready, 1)
            dve.wait_ge(modrow_full, 3)
            for k in range(6):
                src = bank[0][k // 2][0:B, (k % 2) * D:(k % 2 + 1) * D]
                dst = modrow[:, k * D:(k + 1) * D]
                if k in (0, 3):
                    V.tensor_copy(dst, src).then_inc(modrow_ready, 1)
                elif k in (1, 4):
                    V.tensor_scalar(dst, src, 1.0, None, ALU.add).then_inc(modrow_ready, 1)
                else:
                    before = 3 * (k // 3)
                    if k == 5:
                        dve.wait_ge(modrow_ready, 5)
                    V.tensor_scalar(modtmp[:, 0:D], src, 0.0, 2.0, ALU.is_ge, ALU.mult).then_inc(gate_step, 1)
                    V.tensor_scalar(modtmp[:, D:2 * D], src, -1.0, 0.25, ALU.mult, ALU.max).then_inc(gate_step, 1)
                    dve.wait_ge(gate_step, before + 2)
                    V.tensor_tensor(modtmp[:, D:2 * D], src, modtmp[:, D:2 * D], ALU.max).then_inc(gate_step, 1)
                    dve.wait_ge(gate_step, before + 3)
                    V.scalar_tensor_tensor(out=dst, in0=modtmp[:, 0:D], scalar=-1.0, in1=modtmp[:, D:2 * D],
                                           op0=ALU.add, op1=ALU.mult).then_inc(modrow_ready, 1)
            dve.wait_ge(weights_loaded, 16 * WEIGHT_LOADS)
            V.tensor_copy(IDENTB[:], IDENT[:]).then_inc(consts_ready, 1)
            V.tensor_copy(WINDOWB[:].rearrange("p f n -> p (f n)"), windowf).then_inc(consts_ready, 1)
            dve.wait_ge(consts_ready, 11)
            dve.wait_ge(mod_stored, 32)
            for s in range(STREAMS):
                ins = V.memset(qT[s][:], 0.0)
            ins.then_inc(consts_ready, 1)
            dve.wait_ge(factors_ready, 4 * DEPTH)
            dve.wait_ge(consts_ready, NCONST)

            def begin_batch(j):
                V.memset(state[1][:], 0.0).then_inc(state_zeroed[1], 1)
                for s in range(STREAMS):
                    dve.wait_ge(tail_saved[s], j * (16 * DEPTH * TILES) + AHEAD)
                    V.memset(tailcol[s][:], 0.0)
                    V.memset(tailrow[s][:], 0.0).then_inc(tails_zeroed[s], 1)

            def one_pass(order, n, i, na, ja, next_batch):
                links = [0 if order is FIRST else CHAIN_FIRST]

                def link(ins):
                    links[0] += 1
                    ins.then_inc(chain, 1)
                    dve.wait_ge(chain, n[0] * CHAIN + links[0])

                def first_guess(cols):
                    v, r = (RS[:, a, cols] for a in range(2))
                    link(V.tensor_scalar(r.bitcast(I32), v.bitcast(I32), -0.5, MAGIC, ALU.mult, ALU.add))

                def rsqrt(cols, ready=None):
                    first_guess(cols)
                    v, r, t = (RS[:, a, cols] for a in range(3))
                    for k in range(3):
                        link(V.tensor_tensor(t, r, r, ALU.mult))
                        link(V.scalar_tensor_tensor(out=t, in0=t, scalar=-0.5, in1=v, op0=ALU.mult, op1=ALU.mult))
                        ins = V.scalar_tensor_tensor(out=r, in0=t, scalar=1.5, in1=r, op0=ALU.add, op1=ALU.mult)
                        if ready and k == 2:
                            ins.then_inc(ready, 1)
                        else:
                            link(ins)

                def variance(s, parts, between=None):
                    for k, part in enumerate(parts):
                        if k == 1:
                            between()
                        ins = V.bn_stats(st[s][:, k], part)
                    link(ins)
                    V.memset(spare[s][:], 0.0)
                    link(V.bn_aggr(mv[s][:], st[s][:, 0:len(parts)].rearrange("p a b -> p (a b)")))
                    link(V.tensor_scalar(RS[:, 0, LNCOL[s]:LNCOL[s] + 1], mv[s][:, 1:2], EPS_LN, None, ALU.add))

                def scaled(s, parts):
                    at = 0
                    for part in parts:
                        w = part.shape[1]
                        ins = V.tensor_scalar(z[s][:, at:at + w], part, mv[s][:, 0:1], RS[:, 1, LNCOL[s]:LNCOL[s] + 1],
                                              ALU.subtract, ALU.mult)
                        at += w
                    return ins

                def normalise(s, parts, between=None):
                    variance(s, parts, between)
                    v, r, t, minus_half_v = (RS[:, a, LNCOL[s]:LNCOL[s] + 1] for a in range(4))
                    V.tensor_scalar(minus_half_v, mv[s][:, 1:2], EPS_LN, -0.5, ALU.add, ALU.mult)
                    first_guess(slice(LNCOL[s], LNCOL[s] + 1))
                    for _ in range(3):
                        link(V.tensor_scalar(t, r, r, minus_half_v, ALU.mult, ALU.mult))
                        link(V.tensor_scalar(r, t, 1.5, r, ALU.add, ALU.mult))
                    return scaled(s, parts)

                def a_norm(s, l):
                    if s == 0 and next_batch:
                        V.memset(state[s][:], 0.0).then_inc(state_zeroed[s], 1)
                    dve.wait_ge(xin_loaded[s], na[s] * 16 + 16)
                    normalise(s, [xin[s][:]]).then_inc(z_ready[s], 1)

                def a_bias(s, l):
                    wait_filled(dve, s, na, ("A", "qk"))
                    V.tensor_tensor(qkb[s].rearrange("p h d -> p (h d)"), held(s, ("A", "qk"))[:], BA[:, 0:2 * D],
                                    ALU.add).then_inc(drain(s, ("A", "qk")), 1)
                    wait_drained(dve, s, na, ("A", "qk"))
                    V.tensor_scalar(below[s][:], qkb[s][:], 0.0, None, ALU.min).then_inc(below_ready[s], 1)
                    wait_filled(dve, s, na, ("A", "v"))
                    V.tensor_tensor(v1[s][:, :, 0:AD], held(s, ("A", "v"))[:, 0:D].rearrange("p (h d) -> p h d", h=AH),
                                    BA[:, 2 * D:].rearrange("p (h d) -> p h d", h=AH), ALU.add).then_inc(drain(s, ("A", "v")), 1)

                def a_phi(s, l):
                    dve.wait_ge(exp_ready[s], na[s] + 1)
                    V.scalar_tensor_tensor(out=phi[s].rearrange("p q (h d) -> p (q h) d", d=AD), in0=qkb[s][:], scalar=0.0,
                                           in1=ex[s][:], op0=ALU.max, op1=ALU.add).then_inc(phi_ready[s], 1)

                def a_spread(s, l):
                    wait_drained(dve, s, na, ("A", "phi"))
                    for g in range(1, AG, 2):
                        ins = V.tensor_scalar(spreadq[s][:, :, g], phiT[s][:, 0], BLOCKDIAG[:, g * AV:g * AV + 1], None, ALU.mult)
                        if g % (AG // 2) == AG // 2 - 1:
                            ins.then_inc(spread_by_vector[s], 1)

                def a_mask(s, l):
                    for m in range(QUARTERS):
                        key = ("A", f"score{m}")
                        wait_filled(dve, s, na, key)
                        per = AH // QUARTERS
                        V.tensor_tensor(sm[s][:, m * per:(m + 1) * per], held(s, key)[:].rearrange("p (h t) -> p h t", h=per),
                                        CAUSAL[:].unsqueeze(1).to_broadcast((P, per, P)), ALU.mult).then_inc(drain(s, key), 1)

                def a_divide(s, l):
                    key = ("A", "num")
                    wait_filled(dve, s, na, key)
                    num = held(s, key)[:, 0:AH * AV].rearrange("p (h d) -> p h d", h=AH)
                    link(V.tensor_scalar(rd[s][:, 0].unsqueeze(2), num[:, :, AD:AV], EPS_DEN, None, ALU.add))
                    link(V.reciprocal(rd[s][:, 1], rd[s][:, 0]))
                    V.tensor_tensor(oa[s][:], num[:, :, 0:AD], rd[s][:, 1].unsqueeze(2).to_broadcast((P, AH, AD)),
                                    ALU.mult).then_inc(drain(s, key), 1)
                    key = ("A", "kv")
                    wait_filled(dve, s, na, key)
                    V.tensor_tensor(t0[s][:], held(s, key)[:, 0:AH * AV], BLOCKDIAG[:], ALU.mult).then_inc(drain(s, key), 1)
                    wait_drained(dve, s, na, key)
                    V.tensor_tensor(state[s][:], state[s][:], t0[s][:], ALU.add).then_inc(state_ready[s], 1)

                def a_add(s, l):
                    key = ("A", "wo")
                    wait_filled(dve, s, na, key)
                    dve.wait_ge(mod_loaded[s], ja[s] * 32 + 32)
                    V.tensor_tensor(branch[s][:, 0:D], held(s, key)[:, 0:D], BO[:], ALU.add).then_inc(drain(s, key), 1)
                    wait_drained(dve, s, na, key)
                    link(V.tensor_tensor(branch[s][:, 0:D], branch[s][:, 0:D], mod[s][:, 0:D], ALU.mult))
                    V.tensor_tensor(x1[s][:], branch[s][:, 0:D], xin[s][:], ALU.add).then_inc(x1_ready[s], 1)

                def modulate(s, l):
                    dve.wait_ge(x1_ready[s], na[s] + 1)
                    link(normalise(s, [x1[s][:]]))
                    link(V.tensor_tensor(z[s][:], z[s][:], mod[s][:, 2 * D:3 * D], ALU.mult))
                    V.tensor_tensor(xl[s][:], z[s][:], mod[s][:, D:2 * D], ALU.add).then_inc(xl_ready[s], 1)

                def rotate(q, s, l):
                    key = (l, "qk"[q])
                    got = held(s, key)[:]
                    factor = [ROT[:, l, bass.ds(i[s], 1), q, f] for f in range(2)]
                    dve.wait_ge(squares_ready[s], n[s] * (2 * DEPTH) + (2 * l + 2 - q))
                    V.tensor_tensor(rot1[s][:, q], got.rearrange("p (h d) -> p h d", h=LH),
                                    factor[0].to_broadcast((P, LH, LD)), ALU.mult)
                    V.tensor_tensor(rot2[s][:, q].rearrange("p h (b d) -> p h b d", b=2),
                                    got.rearrange("p (h b d) -> p h b d", h=LH, b=2)[:, :, ::-1],
                                    factor[1].rearrange("p o (b d) -> p o b d", b=2).to_broadcast((P, LH, 2, LD // 2)),
                                    ALU.mult).then_inc(drain(s, key), 1)
                    if q == 0:
                        wait_drained(dve, s, n, key)
                        V.tensor_tensor(qk[s][:, 0].rearrange("p a t -> p (a t)"), rot1[s][:, 0].rearrange("p h d -> p (h d)"),
                                        rot2[s][:, 0].rearrange("p h d -> p (h d)"), ALU.add).then_inc(q_ready[s], 1)
                    else:
                        key_norms(s)

                def square_sums(q, s):
                    at = (QCOL, KCOL)[q][s]
                    cols = slice(at, at + LH)
                    link(V.tensor_reduce(RS[:, 0, cols], sq[s][:, q], AX.X, ALU.add))
                    link(V.tensor_scalar(RS[:, 0, cols], RS[:, 0, cols], 1e-24, None, ALU.max))
                    return cols

                def key_norms(s):
                    rsqrt(square_sums(1, s), knorm_ready[s])

                def query_scale(s):
                    cols = slice(QCOL[s], QCOL[s] + LH)
                    link(V.tensor_scalar(RS[:, 3, cols], RS[:, 1, cols], 8.0, None, ALU.mult))

                def query_norms(s, l):
                    cols = square_sums(0, s)
                    if (s, l) == (0, 0):
                        rsqrt(cols)
                        query_scale(s)

                def rowmax(p, s, l):
                    key = (l, f"sim{p}")
                    wait_filled(dve, s, n, key)
                    heads = slice(2 * p, 2 * p + 2)
                    link(V.tensor_reduce(mx[s][:, 0, heads], held(s, key)[:].rearrange("p (e t) -> p e t", e=2),
                                            AX.X, ALU.max))
                    V.scalar_tensor_tensor(out=mx[s][:, 1, heads], in0=mx[s][:, 0, heads], scalar=-1.0,
                                           in1=RS[:, 3, QCOL[s] + 2 * p:QCOL[s] + 2 * p + 2], op0=ALU.mult, op1=ALU.mult).then_inc(negmax_ready[s], 1)

                def turned_p(p, s, l):
                    key = (l, f"p{p}")
                    wait_filled(dve, s, n, key)
                    V.tensor_copy(pT[s][:, p % 2].rearrange("p a t -> p (a t)"), held(s, key)[:]).then_inc(drain(s, key), 1)

                def divide(half, s, l):
                    key = (l, f"o{half}")
                    wait_filled(dve, s, n, key)
                    o = held(s, key)[:, 0:4 * LV].rearrange("p (h d) -> p h d", h=4)
                    link(V.reciprocal(rd[s][:, 0, 0:4].unsqueeze(2), o[:, :, LD:LV]))
                    V.tensor_tensor(on[s].rearrange("p c t -> p (c t)")[:, half * 4 * LD:(half + 1) * 4 * LD].rearrange("p (h d) -> p h d", h=4),
                                    o[:, :, 0:LD], rd[s][:, 0, 0:4].unsqueeze(2).to_broadcast((P, 4, LD)),
                                    ALU.mult).then_inc(drain(s, key), 1)

                def add_attention(s, l):
                    wait_filled(dve, s, n, (l, "wo"))
                    V.tensor_tensor(xl[s][:], xl[s][:], held(s, (l, "wo"))[:, 0:D], ALU.add).then_inc(drain(s, (l, "wo")), 1)

                def norm(s, l):
                    wait_drained(dve, s, n, (l, "wo"))
                    dve.wait_ge(tail_read[s], n[s] * (16 * DEPTH) + 16 * (l + 1))
                    def between():
                        dve.wait_ge(shifted[s], n[s] * (16 * DEPTH) + 16 * (l + 1))

                    parts = [xl[s][:, 0:P], xs2[s][:]]
                    if (s, l) == (1, DEPTH - 1):
                        normalise(s, parts, between).then_inc(z_ready[s], 1)
                    else:
                        variance(s, parts, between)
                        o = 1 - s
                        lo = min(LNCOL[s], QCOL[o])
                        rsqrt(slice(lo, lo + LH + 1))
                        scaled(s, parts).then_inc(z_ready[s], 1)
                        query_scale(o)


                def gates(m, s, l):
                    key = (l, f"ag{m}")
                    dve.wait_ge(gelu_ready[s], n[s] * (HC * DEPTH) + (l * HC + 2 * m + 2))
                    for k in (2 * m, 2 * m + 1):
                        rows = LAST if k == HC - 1 else P
                        b = (l * 2) * HC + k
                        at = 2 * (k % 2) * P
                        ins = V.scalar_tensor_tensor(out=hid[s][0:rows, k], in0=held(s, key)[0:rows, at:at + P],
                                                     scalar=B1[0:rows, b:b + 1], in1=gl[s][0:rows, k],
                                                     op0=ALU.add, op1=ALU.mult)
                    ins.then_inc(drain(s, key), 1)

                def add_ffn(s, l):
                    wait_filled(dve, s, n, (l, "w2"))
                    dve.wait_ge(xb_ready[s], n[s] * DEPTH + (l + 1))
                    dve.wait_ge(tail_saved[s], n[s] * (16 * DEPTH) + (16 * (l + 1) + AHEAD))
                    V.tensor_tensor(xl[s][:], xb[s][:], held(s, (l, "w2"))[:, 0:D], ALU.add).then_inc(drain(s, (l, "w2")), 1)
                    if l == DEPTH - 1:
                        finish(s)

                def finish(s):
                    wait_drained(dve, s, n, (DEPTH - 1, "w2"))
                    dve.wait_ge(y_stored[s], n[s] * 16 + AHEAD)
                    link(V.tensor_tensor(y[s][:], xl[s][:], mod[s][:, 3 * D:], ALU.mult))
                    V.tensor_tensor(y[s][:], y[s][:], x1[s][:], ALU.add).then_inc(y_ready[s], 1)

                def project_a(s, l):
                    a_bias(s, l)
                    a_phi(s, l)

                steps = {"norm_a": a_norm, "project_a": project_a, "turn_phi": a_spread, "scores": a_mask, "numerators": a_divide,
                         "out_a": a_add, "modulate": modulate,
                         "rotate_q": partial(rotate, 0), "project_k": partial(rotate, 1),
                         "turn_q": query_norms, "weigh1": partial(divide, 0), "weigh3": partial(divide, 1),
                         "project_o": add_attention, "norm": norm, "narrow": add_ffn}
                steps.update({f"sim{p}": partial(rowmax, p) for p in range(PAIRS)})
                steps.update({f"turn_p{p}": partial(turned_p, p) for p in range(PAIRS // 2, PAIRS)})
                steps.update({f"gelu{m}": partial(gates, m) for m in range(HC // 2)})
                issue(order, steps)
                assert links[0] == (CHAIN_FIRST if order is FIRST else CHAIN_FIRST + CHAIN), links

            run_passes(dve, one_pass, begin_batch)
        @block.gpsimd
        def _(pool):
            G = nc.gpsimd
            pool.wait_ge(consts_ready, NCONST)
            pool.wait_ge(rotary_loaded, 16 * DEPTH)
            pool.wait_ge(weights_loaded, 16 * WEIGHT_LOADS)
            for l in range(DEPTH):
                for q in range(2):
                    for f in range(2):
                        fac = ROT[:, l, :, q, f].rearrange("p t (b d) -> p t b d", b=2)
                        sc = scales[:, l, q].rearrange("p (b d) -> p b d", b=2)
                        if f == 1:
                            sc = sc[:, ::-1]
                        G.tensor_tensor(fac, fac, sc.unsqueeze(1).to_broadcast((P, TILES, 2, LD // 2)), ALU.mult).then_inc(factors_ready, 1)
            def one_pass(order, n, i, na, ja, next_batch):

                def rotate_k(s, l):
                    wait_drained(pool, s, n, (l, "k"))
                    k = qk[s][:, 1].rearrange("p a t -> p (a t)")
                    G.tensor_tensor(k, rot1[s][:, 1].rearrange("p h d -> p (h d)"), rot2[s][:, 1].rearrange("p h d -> p (h d)"),
                                    ALU.add).then_inc(ksum_ready[s], 1)
                    pool.wait_ge(ksum_ready[s], n[s] * DEPTH + (l + 1))
                    pool.wait_ge(knorm_ready[s], n[s] * DEPTH + (l + 1))
                    k = k.rearrange("p (h d) -> p h d", h=LH)
                    G.tensor_tensor(k, k, RS[:, 1, KCOL[s]:KCOL[s] + LH].unsqueeze(2).to_broadcast((P, LH, LD)), ALU.mult).then_inc(k_ready[s], 1)

                def move_kv(s, l):
                    wait_filled(pool, s, n, (l, "o1"))
                    G.tensor_tensor(kprev[s][:, l], kT[s][:], ZERO[:].unsqueeze(2).to_broadcast((P, PAIRS, P)),
                                    ALU.add).then_inc(kv_moved[s], 1)
                    G.tensor_scalar(vprev[s][:, l], vw[s][:], 1.0, 0.0, ALU.mult, ALU.add).then_inc(kv_moved[s], 1)

                def add_b2(s, l):
                    wait_drained(pool, s, n, (l, "wo"))
                    G.tensor_tensor(xb[s][:], xl[s][:], B2[:, l * D:(l + 1) * D], ALU.add).then_inc(xb_ready[s], 1)

                issue(order, {"project_k": rotate_k, "weigh3": move_kv, "project_o": add_b2})

            run_passes(pool, one_pass)


def kernel(**inputs):
    import concourse.bacc as bacc
    from concourse.bass_utils import run_bass_kernel_spmd

    def of(name):
        return np.ascontiguousarray(inputs[name])

    x = of("L0_attn_x")
    B, N, _ = x.shape
    R, T = B // STREAMS, N // P
    xt = x.reshape(R, STREAMS, T, P, D).transpose(1, 0, 2, 3, 4).reshape(STREAMS, R * T, P, D)
    xt = np.concatenate([xt, np.zeros((STREAMS, 2, P, D), x.dtype)], axis=1)

    f4 = np.float32
    half = np.arange(0, LD, 2, dtype=f4)
    inv_freq = (f4(1.0) / np.power(f4(10000.0), half / f4(LD))).astype(f4)
    t = np.arange(N, dtype=f4)
    freqs = (t[:, None] * inv_freq[None, :]).astype(f4).astype(np.float64)
    base = ((half + f4(0.4 * LD)) / f4(1.4 * LD)).astype(np.float64)
    power = (t.astype(np.float64) - N // 2) / float(WINDOW // 2)
    scale = base[None, :] ** power[:, None]
    cos, sin = np.cos(freqs), np.sin(freqs)
    rot = np.empty((N, 2, 2, LD), f4)
    for q, sc in enumerate((scale, 1.0 / scale)):
        rot[:, q, 0] = np.concatenate([cos * sc, cos * sc], axis=1)
        rot[:, q, 1] = np.concatenate([-sin * sc, sin * sc], axis=1)
    rot = rot.reshape(T, P, 2 * 2 * LD).transpose(1, 0, 2).reshape(P, T * 4 * LD)

    r = np.arange(P)
    blockdiag = np.zeros((P, KC, AG, AV), f4)
    for g in range(AG):
        blockdiag[g * AD:(g + 1) * AD, :, g] = 1.0
    prev = np.where(r[None, :] >= r[:, None], 0.0, MASKED)
    this = np.where(r[None, :] <= r[:, None], 0.0, MASKED)
    window = np.empty((P, 2, 2, 2, WINDOW), f4)
    window[:, 0, :, 0] = MASKED
    window[:, 1, :, 0] = prev[:, None, :]
    window[:, :, :, 1] = this[:, None, None, :]

    def columns(v, chunks):
        return v.reshape(v.shape[0], v.shape[1], chunks, P).transpose(3, 0, 1, 2).reshape(P, -1)

    b1 = np.zeros((DEPTH, 2, HC * P), f4)
    b1[:, :, 0:HID] = of("L0_ffn_b1").reshape(DEPTH, 2, HID)
    arrays = {
        "x": xt,
        "waT": np.concatenate([of(f"L0_attn_W{k}").T for k in "qkv"], axis=1),
        "woaT": of("L0_attn_Wo").T,
        "ba": np.concatenate([of(f"L0_attn_b{k}") for k in "qkv"])[None],
        "bo": of("L0_attn_bo")[None],
        "wqkv": of("L0_ffn_wqkv"), "qs": of("L0_ffn_q_scale"), "ks": of("L0_ffn_k_scale"), "wo": of("L0_ffn_wo"),
        "ln_g": columns(np.stack([of("L0_ffn_ln_g"), of("L0_ffn_ln_b")], axis=1), KC), "ln_b": of("L0_ffn_ln_b"),
        "w1": of("L0_ffn_w1"), "b1": columns(b1, HC), "w2": of("L0_ffn_w2"), "b2": of("L0_ffn_b2").reshape(1, -1),
        "cT": of("L0_c").T, "wmod": of("L0_wmod"),
        "rotary": rot, "ident": np.eye(P, dtype=f4), "causal": (r[:, None] <= r[None, :]).astype(f4),
        "blockdiag": blockdiag.reshape(P, -1), "window": window.reshape(P, -1),
    }
    arrays = {f"in_{k}": np.ascontiguousarray(v) for k, v in arrays.items()}

    nc = bacc.Bacc("TRN2", target_bir_lowering=False, num_devices=1)
    args = [nc.dram_tensor(k, v.shape, mybir.dt.from_np(v.dtype), kind="ExternalInput").ap() for k, v in arrays.items()]
    out = nc.dram_tensor("out_x", (STREAMS, R * T, P, D), F32, kind="ExternalOutput").ap()
    adaln_block(nc, *args, out)
    got = run_bass_kernel_spmd(nc, [arrays], core_ids=[0]).results[0]["out_x"]
    return got.reshape(STREAMS, R, T, P, D).transpose(1, 0, 2, 3, 4).reshape(B, N, D)
```
